# Optimizing a Trainium2 kernel written in Bass

```python
import numpy as np
import jax
import jax.numpy as jnp

def _softmax(x, axis=-1):
    return jax.nn.softmax(x, axis=axis)
def _gelu(x):
    return jax.nn.gelu(x, approximate=True)
def _silu(x):
    return jax.nn.silu(x)
def _sigmoid(x):
    return jax.nn.sigmoid(x)
def _layernorm(x, axis=-1, eps=1e-5):
    m = jnp.mean(x, axis=axis, keepdims=True)
    v = jnp.var(x, axis=axis, keepdims=True)
    return (x - m) / jnp.sqrt(v + eps)
def _scatter_add(tgt, idx, src, axis=0):
    return tgt.at[idx].add(src)
def _segment_sum(src, seg, n):
    return jax.ops.segment_sum(src, seg, n)

kernel_name = 'mk_conv_preact_d2_conv_nchw256_7aa2aa'

def setup_inputs(seed: int = 0):
    np.random.seed(seed)
    _w = jnp.asarray
    def _rec_inputs():
        import jax
        import jax.numpy as jnp
        _gk = jax.random.key(seed)
        x = -0.000125 + 0.9999 * jax.random.normal(jax.random.fold_in(_gk, 1), (8, 256, 128, 128), jnp.float32)
        return x
    x = _rec_inputs()
    def _L0_conv_setup():
        import jax, jax.numpy as jnp
        import numpy as np
        B, DIM, H, W = (8, 256, 128, 128)
        P = 4
        HEADS = 8
        HD = DIM // HEADS
        CPB_HIDDEN = 512

        def _rpe_bias(Hp, Wp, cpb_w1, cpb_b1, cpb_w2):
            rh = (jnp.arange(2 * Hp - 1, dtype=jnp.float32) - (Hp - 1)) / max(Hp - 1, 1)
            rw = (jnp.arange(2 * Wp - 1, dtype=jnp.float32) - (Wp - 1)) / max(Wp - 1, 1)
            rel = jnp.stack(jnp.meshgrid(rh, rw, indexing='ij'), axis=-1).reshape(-1, 2)
            table = jax.nn.relu(rel @ cpb_w1.T + cpb_b1) @ cpb_w2.T
            ch = np.arange(Hp)
            cw = np.arange(Wp)
            coords = np.stack(np.meshgrid(ch, cw, indexing='ij')).reshape(2, -1)
            d = coords[:, :, None] - coords[:, None, :]
            idx = (d[0] + Hp - 1) * (2 * Wp - 1) + (d[1] + Wp - 1)
            bias = table[jnp.asarray(idx)]
            return bias.transpose(2, 0, 1)
        key = jax.random.key(seed)
        ks = jax.random.split(key, 12)
        s = 0.02
        return {'x': jax.random.normal(ks[0], (B, DIM, H, W), dtype=jnp.float32), 'w_embed': jax.random.normal(ks[1], (DIM, DIM, P, P), dtype=jnp.float32) * s, 'b_embed': jnp.zeros((DIM,), dtype=jnp.float32), 'cpb_w1': jax.random.normal(ks[2], (CPB_HIDDEN, 2), dtype=jnp.float32) * s, 'cpb_b1': jnp.zeros((CPB_HIDDEN,), dtype=jnp.float32), 'cpb_w2': jax.random.normal(ks[3], (HEADS, CPB_HIDDEN), dtype=jnp.float32) * s, 'w_qkv': jax.random.normal(ks[4], (3 * DIM, DIM), dtype=jnp.float32) * s, 'b_qkv': jnp.zeros((3 * DIM,), dtype=jnp.float32), 'w_proj': jax.random.normal(ks[5], (DIM, DIM), dtype=jnp.float32) * s, 'b_proj': jnp.zeros((DIM,), dtype=jnp.float32), 'w_unembed': jax.random.normal(ks[6], (DIM, DIM, P, P), dtype=jnp.float32) * s, 'b_unembed': jnp.zeros((DIM,), dtype=jnp.float32)}
    _L0_conv_all = _L0_conv_setup()
    _L0_conv_in = {k: v for k, v in _L0_conv_all.items() if k in ('w_embed', 'b_embed', 'cpb_w1', 'cpb_b1', 'cpb_w2', 'w_qkv', 'b_qkv', 'w_proj', 'b_proj', 'w_unembed', 'b_unembed', )}
    del _L0_conv_all

    def _L1_conv_setup():
        import jax, jax.numpy as jnp
        import numpy as np
        import math
        FREQ_SEL = [(0, 0), (0, 1), (1, 0), (1, 1)]

        def _dct_mat(N):
            i = np.arange(N, dtype=np.float32)[:, None]
            j = np.arange(N, dtype=np.float32)[None, :]
            A = np.cos(math.pi * j * (2.0 * i + 1.0) / (2.0 * N)) * math.sqrt(2.0 / N)
            A[0] *= math.sqrt(0.5)
            return jnp.asarray(A, dtype=jnp.float32)

        def _basis(H, W):
            A_H = _dct_mat(H)
            A_W = _dct_mat(W)
            planes = [A_H[u][:, None] * A_W[v][None, :] for u, v in FREQ_SEL]
            return jnp.stack(planes, axis=0)
        key = jax.random.key(seed)
        k1, k2, k3 = jax.random.split(key, 3)
        B, C, H, W = (32, 256, 64, 64)
        hidden = C // 4
        x = jax.random.normal(k1, (B, C, H, W), dtype=jnp.float32)
        w1 = jax.random.normal(k2, (hidden, C), dtype=jnp.float32) * (1.0 / math.sqrt(C))
        w2 = jax.random.normal(k3, (C, hidden), dtype=jnp.float32) * (1.0 / math.sqrt(hidden))
        return {'x': x, 'w1': w1, 'w2': w2}
    _L1_conv_all = _L1_conv_setup()
    _L1_conv_in = {k: v for k, v in _L1_conv_all.items() if k in ('w1', 'w2', )}
    del _L1_conv_all

    return {
        "x": x,
        "L0_conv_w_embed": _L0_conv_in["w_embed"],
        "L0_conv_b_embed": _L0_conv_in["b_embed"],
        "L0_conv_cpb_w1": _L0_conv_in["cpb_w1"],
        "L0_conv_cpb_b1": _L0_conv_in["cpb_b1"],
        "L0_conv_cpb_w2": _L0_conv_in["cpb_w2"],
        "L0_conv_w_qkv": _L0_conv_in["w_qkv"],
        "L0_conv_b_qkv": _L0_conv_in["b_qkv"],
        "L0_conv_w_proj": _L0_conv_in["w_proj"],
        "L0_conv_b_proj": _L0_conv_in["b_proj"],
        "L0_conv_w_unembed": _L0_conv_in["w_unembed"],
        "L0_conv_b_unembed": _L0_conv_in["b_unembed"],
        "L1_conv_w1": _L1_conv_in["w1"],
        "L1_conv_w2": _L1_conv_in["w2"],
    }

def reference(x, L0_conv_w_embed, L0_conv_b_embed, L0_conv_cpb_w1, L0_conv_cpb_b1, L0_conv_cpb_w2, L0_conv_w_qkv, L0_conv_b_qkv, L0_conv_w_proj, L0_conv_b_proj, L0_conv_w_unembed, L0_conv_b_unembed, L1_conv_w1, L1_conv_w2):
    import jax
    import jax.numpy as jnp
    def _L0_conv_ref(x, w_embed, b_embed, cpb_w1, cpb_b1, cpb_w2, w_qkv, b_qkv, w_proj, b_proj, w_unembed, b_unembed):
        import jax, jax.numpy as jnp
        import numpy as np
        B, DIM, H, W = (8, 256, 128, 128)
        P = 4
        HEADS = 8
        HD = DIM // HEADS
        CPB_HIDDEN = 512

        def _rpe_bias(Hp, Wp, cpb_w1, cpb_b1, cpb_w2):
            rh = (jnp.arange(2 * Hp - 1, dtype=jnp.float32) - (Hp - 1)) / max(Hp - 1, 1)
            rw = (jnp.arange(2 * Wp - 1, dtype=jnp.float32) - (Wp - 1)) / max(Wp - 1, 1)
            rel = jnp.stack(jnp.meshgrid(rh, rw, indexing='ij'), axis=-1).reshape(-1, 2)
            table = jax.nn.relu(rel @ cpb_w1.T + cpb_b1) @ cpb_w2.T
            ch = np.arange(Hp)
            cw = np.arange(Wp)
            coords = np.stack(np.meshgrid(ch, cw, indexing='ij')).reshape(2, -1)
            d = coords[:, :, None] - coords[:, None, :]
            idx = (d[0] + Hp - 1) * (2 * Wp - 1) + (d[1] + Wp - 1)
            bias = table[jnp.asarray(idx)]
            return bias.transpose(2, 0, 1)
        Bx, C, Hf, Wf = x.shape
        Hp, Wp = (Hf // P, Wf // P)
        N = Hp * Wp
        xr = x.reshape(Bx, C, Hp, P, Wp, P)
        z = jnp.einsum('bchpwq,ocpq->bohw', xr, w_embed) + b_embed[None, :, None, None]
        bias = _rpe_bias(Hp, Wp, cpb_w1, cpb_b1, cpb_w2)
        tok = z.reshape(Bx, C, N).transpose(0, 2, 1)
        qkv = tok @ w_qkv.T + b_qkv
        qkv = qkv.reshape(Bx, N, 3, HEADS, HD).transpose(2, 0, 3, 1, 4)
        q, k, v = (qkv[0], qkv[1], qkv[2])
        scale = HD ** (-0.5)
        attn = jnp.einsum('bhnd,bhmd->bhnm', q * scale, k) + bias[None]
        attn = jax.nn.softmax(attn, axis=-1)
        out = jnp.einsum('bhnm,bhmd->bhnd', attn, v)
        out = out.transpose(0, 2, 1, 3).reshape(Bx, N, C)
        out = out @ w_proj.T + b_proj
        z2 = out.transpose(0, 2, 1).reshape(Bx, C, Hp, Wp)
        y = jnp.einsum('bchw,copq->bohpwq', z2, w_unembed)
        y = y.reshape(Bx, C, Hf, Wf) + b_unembed[None, :, None, None]
        return y

    def _L1_conv_ref(x, w1, w2):
        import jax, jax.numpy as jnp
        import numpy as np
        import math
        FREQ_SEL = [(0, 0), (0, 1), (1, 0), (1, 1)]

        def _dct_mat(N):
            i = np.arange(N, dtype=np.float32)[:, None]
            j = np.arange(N, dtype=np.float32)[None, :]
            A = np.cos(math.pi * j * (2.0 * i + 1.0) / (2.0 * N)) * math.sqrt(2.0 / N)
            A[0] *= math.sqrt(0.5)
            return jnp.asarray(A, dtype=jnp.float32)

        def _basis(H, W):
            A_H = _dct_mat(H)
            A_W = _dct_mat(W)
            planes = [A_H[u][:, None] * A_W[v][None, :] for u, v in FREQ_SEL]
            return jnp.stack(planes, axis=0)
        B, C, H, W = x.shape
        basis = _basis(H, W)
        spectral = jnp.einsum('bchw,fhw->bcf', x, basis)
        y = jnp.einsum('bcf,hc->bhf', spectral, w1)
        y = jax.nn.relu(y)
        y = jnp.einsum('bhf,ch->bcf', y, w2)
        gate = jax.nn.sigmoid(jnp.mean(y, axis=-1))
        return x * gate[:, :, None, None]

    def _gn(v, G=32, eps=1e-5):
        B_, C_, H_, W_ = v.shape
        g = v.reshape(B_, G, C_ // G, H_, W_)
        m = jnp.mean(g, axis=(2, 3, 4), keepdims=True)
        s = jnp.var(g, axis=(2, 3, 4), keepdims=True)
        return ((g - m) / jnp.sqrt(s + eps)).reshape(v.shape)

    def _ln_c(v, eps=1e-6):
        m = jnp.mean(v, axis=1, keepdims=True)
        s = jnp.var(v, axis=1, keepdims=True)
        return (v - m) / jnp.sqrt(s + eps)

    def _ln_t(v, eps=1e-5):
        m = jnp.mean(v, axis=-1, keepdims=True)
        s = jnp.var(v, axis=-1, keepdims=True)
        return (v - m) / jnp.sqrt(s + eps)

    def _to_tokens(v):
        B_, C_, H_, W_ = v.shape
        return v.reshape(B_, C_, H_ * W_).transpose(0, 2, 1)
    def _from_tokens(t, like):
        B_, C_, H_, W_ = like.shape
        return t.transpose(0, 2, 1).reshape(B_, C_, H_, W_)

    x = x + _L0_conv_ref(_gn(x), L0_conv_w_embed, L0_conv_b_embed, L0_conv_cpb_w1, L0_conv_cpb_b1, L0_conv_cpb_w2, L0_conv_w_qkv, L0_conv_b_qkv, L0_conv_w_proj, L0_conv_b_proj, L0_conv_w_unembed, L0_conv_b_unembed)
    x = x + _L1_conv_ref(_gn(x), L1_conv_w1, L1_conv_w2)
    return x


_drawn_inputs = setup_inputs


def setup_inputs(seed=0):
    import zlib

    import numpy as np

    out = dict(_drawn_inputs(seed))
    spreads = {'L0_conv_b_embed': (0.0, 0.8),
     'L0_conv_cpb_b1': (0.0, 2.0),
     'L0_conv_b_qkv': (0.0, 0.749),
     'L0_conv_b_proj': (0.0, 2.0),
     'L0_conv_b_unembed': (0.0, 0.8)}
    factors = {'L0_conv_w_embed': 8.0,
     'L0_conv_cpb_w1': 59.08,
     'L0_conv_cpb_w2': 64.0,
     'L0_conv_w_qkv': 8.0,
     'L0_conv_w_proj': 4.922,
     'L1_conv_w1': 8.0,
     'L1_conv_w2': 6.636}
    for name, (base, spread) in spreads.items():
        noise = np.random.default_rng([zlib.crc32(name.encode()), seed]).standard_normal(out[name].shape)
        drawn = base * np.exp(spread * noise) if base else spread * noise
        out[name] = jnp.asarray(drawn.astype(out[name].dtype))
    for name, factor in factors.items():
        out[name] = (out[name] * factor).astype(out[name].dtype)
    return out
```

```python
import concourse.bass as bass
from concourse import mybir
from contextlib import ExitStack

B, C, H, W = 8, 256, 128, 128
PT = 4
HP, WP_ = H // PT, W // PT
N = HP * WP_
NH_, HD = 8, 32
HID = C // 4
CPB = 512
REL = 2 * HP - 1
UB = (2 * HP - PT) * WP_
GN_EPS = 1e-5


def build(nc, a, plane_sums):
    f32, f32r, bf16 = mybir.dt.float32, mybir.dt.float32r, mybir.dt.bfloat16
    ALU, ACT = mybir.AluOpType, mybir.ActivationFunctionType
    AX = mybir.AxisListType
    SCALE = float(HD) ** -0.5

    d_we = nc.dram_tensor("split_embed", [8, 2, 128, 2, 512], f32, kind="Internal").ap()
    d_wu = nc.dram_tensor("split_unembed", [2, 4, 2, 128, 2, 2, 2, 128], f32, kind="Internal").ap()
    d_tab = nc.dram_tensor("bias_table", [2, NH_, REL * REL], f32, kind="Internal").ap()
    d_bt = nc.dram_tensor("bias_split", [NH_, 128, 2, UB], f32, kind="Internal").ap()
    d_mt = nc.dram_tensor("bias_for_max", [NH_, 128, UB], bf16, kind="Internal").ap()

    x, out = a["x"], a["out"]
    xv = x.rearrange("b c (hp p) w -> b c hp p w", p=PT)

    ctx = ExitStack()
    with ctx:
        def region(*layouts):
            seen, most = {}, 0
            for layout in layouts:
                with ExitStack() as piece:
                    size = 0
                    for name, shape, dt in layout:
                        seen[name] = piece.enter_context(nc.sbuf_tensor(name, shape, dt))
                        k = 2 if dt == bf16 else 4
                        for s in shape[1:]:
                            k *= s
                        size += (k + 31) // 32 * 32
                    most = max(most, size)
            ctx.enter_context(nc.sbuf_tensor("hold_" + layouts[0][0][0], [128, most // 4], f32))
            return seen

        r = region(
            [("x1", [128, 2, H * W], f32)],
            [("bias_t", [128, 2, 2, 2, UB], f32r), ("max_t0", [128, UB], bf16),
             ("q_stack", [128, NH_, N], f32r), ("k_stack", [128, NH_, N], f32r)],
            [("qk", [128, 4, N], f32), ("qk_h", [128, 4, N], f32r), ("qk_l", [128, 4, N], f32r)],
            [("raw", [128, 2, UB], f32), ("raw_h", [128, 2, UB], f32r), ("raw_l", [128, 2, UB], f32r),
             ("rel", [3, REL * REL], f32), ("hid", [128, 2, 512], f32), ("tab", [NH_, REL * REL], f32),
             ("tab_rev", [NH_, REL * REL], f32), ("cpb1", [3, CPB], f32), ("cpb2", [128, 4, NH_], f32),
             ("raw_m", [128, 2, UB], bf16), ("ident0", [128, 128], f32)])
        x1, bias_t, q_stack, k_stack = r["x1"], r["bias_t"], r["q_stack"], r["k_stack"]
        qk, qk_h, qk_l = r["qk"], r["qk_h"], r["qk_l"]
        pro = r
        x1v = x1[:, :, :].rearrange("c o (hp p wp q) -> c o p q hp wp", p=PT, wp=WP_, q=PT)
        x1r = x1[:, :, :].rearrange("c o (hp p w) -> c o p hp w", p=PT, w=W)
        xs = region([("x_stream", [128, 2, 2048], f32)])["x_stream"]
        r = region([("x1_rows", [128, 2, 8, W], f32)], [("mlp1", [128, 2, HID], f32), ("mlp2", [HID, C], f32)])
        x1t, mlp1, mlp2 = r["x1_rows"], r["mlp1"], r["mlp2"]
        r = region([("x_split", [128, 2, 2, 2, 512], f32r)],
                   [("prob", [128, 2, 1024], f32), ("v", [128, 8, NH_, 2 * HD], f32)],
                   [("pad", [128, 2048], f32), ("z2", [128, 2, 2, N], f32r)])
        x_split, prob, v, z2 = r["x_split"], r["prob"], r["v"], r["z2"]
        r = region([("w_ring", [128, 4, 1024], f32r)],
                   [("w_qkv", [128, 2, 3 * C], f32), ("w_proj", [128, 2, C], f32), ("max_t1", [128, UB], bf16)])
        w_ring, w_qkv, w_proj = r["w_ring"], r["w_qkv"], r["w_proj"]
        max_t = [pro["max_t0"], r["max_t1"]]
        z = region([("z", [128, 2, N], f32)])["z"]
        rows = region([("rows", [128, 512], f32)])["rows"]
        r = region([("row_sums", [128, 2, 2, W], f32)], [("dump", [128, N], bf16)])
        row_sums, dump = r["row_sums"], r["dump"]

        def sb(name, shape, dt=f32):
            return ctx.enter_context(nc.sbuf_tensor(name, shape, dt))

        ident = sb("ident", [128, 128], f32r)
        group = sb("group", [128, 128])
        cos_w = sb("cos_w", [128, 2, W])
        cos_h = sb("cos_h", [128, 32])
        bn = sb("bn", [128, 32, 6])
        neg_max = sb("neg_max", [16, 128], f32r)
        mx = sb("mx", [128, 2, 16])
        vec = sb("vec", [128, 64])
        b_embed, b_un, b_proj, b_v = (vec[:, 2 * i:2 * i + 2] for i in range(4))
        b_qk = vec[:, 8:12]
        b_qks = vec[:, 12:16]
        mv = vec[:, 16:20].rearrange("p (c t) -> p c t", t=2)
        dev, var, veps, power = (vec[:, 20 + 2 * i:22 + 2 * i] for i in range(4))
        rstd, shift = vec[:, 28:30], vec[:, 30:32]
        spec = vec[:, 32:40].rearrange("p (o f) -> p o f", f=4)
        gsum, gexp, gate, gr = (vec[:, 40 + 2 * i:42 + 2 * i] for i in range(4))
        scale1, shift1 = vec[:, 48:50], vec[:, 50:52]
        hidden = vec[0:HID, 52:56]
        rstd1, negm1 = vec[:, 56:58], vec[:, 58:60]
        mean, gneg = vec[:, 60:62], vec[:, 62:64]

        PS = [ctx.enter_context(nc.psum_tensor(f"wide{i}", [128, 1024], f32)) for i in range(3)]
        PB = [ctx.enter_context(nc.psum_tensor(f"bank{i}", [128, 512], f32)) for i in range(2)]
        small = PS[2]

        def sem(name):
            return ctx.enter_context(nc.semaphore(name))

        s = {}
        for name in (
            "const_in raw_in0 raw_in1 raw_out0 raw_out1 tab_out xs_in0 xs_in1 w_in0 w_in1 w_in2 w_in3 "
            "wqkv_in stack_in bias_in0 bias_in1 maxt_in0 maxt_in1 nmax_in "
            "xr_in0 xr_in1 xr_in2 xr_in3 xr_in4 xr_in5 xr_in6 xr_in7 rows_in sums_in mlp_in out_done "
            "ident_done raw_h_done raw_l_done hid_mm hid_done tab_mm tab_done rev_done bp_mm prep "
            "split_used qk_mm v_mm smax_mm tr_mm score_mm prob_used proj_mm un_mm rows_mm "
            "gm_mm gv_mm gm1_mm gv1_mm y1_mm y2_mm "
            "norm_done z_done qk_done v_done exp_done z2h_done rows_done hid1_done gexp_done "
            "h_done split_done qkh_done qks_done max_done nmax_done recip_done o_done z2_done x1_done bn_done "
            "chunk_done stat_done dev_done veps_done coef_done mv1_done dev1_done veps1_done spec_link spec_done gate_link gate_done "
            "ones_done kone_done power_done rstd_done rstd1_done final_done passed"
        ).split():
            s[name] = sem(name)

        block = ctx.enter_context(nc.Block())

        def positive(count):
            return not isinstance(count, int) or count > 0

        def max_tiles(step):
            return min(16, 2 * (step + 1) if step < 4 else step + 5)

        RAW = 8 + 8 + NH_ + NH_
        RAW_LOW = 8 + 8 + NH_

        def first(b):
            return isinstance(b, int) and b == 0

        def batches(eng, step):
            step(0, True)
            with eng.Fori(1, B - 1) as b:
                step(b, True)
            step(B - 1, False)

        def raw_in_total(n):
            return 16 * sum(1 if m < 16 else 4 if m < RAW_LOW else 4 for m in range(n % 2, n + 1, 2))

        def raw_out_total(sl, count):
            return 16 * sum(2 if m < 8 else 8 if m < 16 else 2 if m < RAW_LOW else 1 for m in range(sl, count, 2))

        def raw_width(n):
            return 1024 if n < 16 else UB

        def raw_part(n):
            part = pro["raw"][:, n % 2, 0:raw_width(n)]
            return part if n < 16 else part[:, ::-1]

        @block.sync
        def _(sp):
            def const(dst, src):
                sp.dma_start(dst, src).then_inc(s["const_in"], 16)

            const(pro["ident0"][:, :], a["identity"])
            const(group[:, :], a["group_mean"])
            const(cos_w[:, :, :], a["cos_w"])
            const(cos_h[:, :], a["cos_h"])
            const(pro["rel"][:, :], a["rel"])
            const(pro["cpb1"][0:2, :], a["cpb_w1t"])
            const(pro["cpb1"][2:3, :], a["cpb_b1"])
            const(pro["cpb2"][:, :, :], a["cpb_w2t"].rearrange("(t p) h -> p t h", p=128))
            const(b_embed, a["b_embed"])
            const(b_un, a["b_unembed"])
            const(b_proj, a["b_proj"])
            const(b_v, a["b_v"])
            const(b_qk, a["b_qk"])
            sp.dma_start(w_proj[:, :, :], a["w_projt"].rearrange("(k p) o -> p k o", p=128)).then_inc(s["wqkv_in"], 16)

            def raw_load(n):
                sl = n % 2
                inc = s[f"raw_in{sl}"]
                if n >= 2:
                    sp.wait_ge(s["raw_h_done"], n - 1)
                    sp.wait_ge(s["raw_l_done"], min(n - 1, RAW_LOW))
                raw = pro["raw"][:, sl, :]
                if n < 16:
                    w = a["w_embed"] if n < 8 else a["w_unembed"]
                    ch, p = divmod(n % 8, 4)
                    sp.dma_start(raw[:, 0:1024], w[ch * 128:ch * 128 + 128, p, :]).then_inc(inc, 16)
                    return
                if n == 16:
                    sp.wait_ge(s["tab_out"], 32)
                t, h = divmod(n - 16, NH_)
                for i in range(4):
                    src = bass.AP(d_tab.tensor, ((1 - t) * NH_ + h) * REL * REL + i * REL,
                                  [[1, 32], [REL, UB // WP_], [1, WP_]])
                    sp.dma_start(raw[32 * i:32 * i + 32, :].rearrange("p (r c) -> p r c", c=WP_), src)\
                        .then_inc(inc, 16)

            def raw_store(n):
                sl = n % 2
                inc = s[f"raw_out{sl}"]
                sp.wait_ge(s["raw_h_done"], n + 1)
                if n < RAW_LOW:
                    sp.wait_ge(s["raw_l_done"], n + 1)
                hl = (pro["raw_h"][:, sl, :].bitcast(f32), pro["raw_l"][:, sl, :].bitcast(f32))
                ch, p = divmod(n % 8, 4)
                for t in range(2):
                    if n < 8:
                        sp.dma_start(d_we[n].rearrange("q c t w -> t c q w")[t],
                                     hl[t][:, 0:1024].rearrange("c (q w) -> c q w", q=2)).then_inc(inc, 16)
                    elif n < 16:
                        src = hl[t][:, 0:1024].rearrange("c (q o k) -> c q o k", o=2, k=128)
                        for oh in range(2):
                            for qp in range(2):
                                sp.dma_start(d_wu[oh, p, qp, :, t, ch, :, :], src[:, 2 * qp:2 * qp + 2, oh, :])\
                                    .then_inc(inc, 16)
                    elif n < RAW_LOW:
                        sp.dma_start(d_bt[n - 16, :, t, :], hl[t]).then_inc(inc, 16)
                    elif t == 0:
                        sp.dma_start(d_mt[n - RAW_LOW], pro["raw_m"][:, sl, :]).then_inc(inc, 16)

            raw_load(0)
            for n in range(RAW):
                if n == 15:
                    sp.wait_ge(s["tab_done"], 8)
                    sp.dma_start(d_tab[0], pro["tab"][:, :]).then_inc(s["tab_out"], 16)
                    sp.wait_ge(s["rev_done"], 1)
                    sp.dma_start(d_tab[1], pro["tab_rev"][:, :]).then_inc(s["tab_out"], 16)
                if n + 1 < RAW:
                    raw_load(n + 1)
                raw_store(n)
            for sl in range(2):
                sp.wait_ge(s[f"raw_out{sl}"], raw_out_total(sl, RAW))


            def load_stats(b, k):
                if k >= 2:
                    sp.wait_ge(s["chunk_done"], 16 * b + k - 1)
                elif not first(b):
                    sp.wait_ge(s["split_done"], 32 * (b - 1) + 2 * (14 + k) + 2)
                dst, inc = xs[:, k % 2, :], s[f"xs_in{k % 2}"]
                ch, kk = divmod(k, 8)
                src = x[b, ch * 128:ch * 128 + 128, kk * 16:kk * 16 + 16, :]
                sp.dma_start(dst.rearrange("c (h w) -> c h w", w=W), src).then_inc(inc, 16)

            def load_embed_x(b, k):
                if k >= 2:
                    sp.wait_ge(s["split_done"], 32 * b + 2 * (k - 2) + 2)
                else:
                    sp.wait_ge(s["chunk_done"], 16 * b + 15 + k)
                dst, inc = xs[:, k % 2, :], s[f"xs_in{k % 2}"]
                (ch, p), nh = divmod(k // 2, 4), k % 2
                src = xv[b, ch * 128:ch * 128 + 128, nh * 16:nh * 16 + 16, p, :]
                sp.dma_start(dst.rearrange("c (h w) -> c h w", w=W), src).then_inc(inc, 16)

            def load_embed_w(b, w):
                i, qp = divmod(w, 2)
                if w >= 4:
                    sp.wait_ge(s["split_used"], 32 * b + 4 * (i - 2) + 3 + qp)
                elif not first(b):
                    last = 12 + (w + 1) % 4
                    sp.wait_ge(s["un_mm"], 32 * (b - 1) + 2 * last + 2)
                else:
                    sp.wait_ge(s["bp_mm"], 1)
                sp.dma_start(w_ring[:, w % 4, :].bitcast(f32), d_we[i, qp].rearrange("c t w -> c (t w)"))\
                    .then_inc(s[f"w_in{w % 4}"], 16)

            def load_un_w(b, w):
                if w >= 4:
                    sp.wait_ge(s["un_mm"], 32 * b + 2 * (w - 4) + 2)
                elif w in (1, 2):
                    sp.wait_ge(s["proj_mm"], 2 * b + 2)
                elif w == 3:
                    sp.wait_ge(s["max_done"], 64 * b + 64)
                (oh, p), qp = divmod(w // 2, 4), w % 2
                sl = (w + 3) % 4
                sp.dma_start(w_ring[:, sl, :].bitcast(f32), d_wu[oh, p, qp].rearrange("c t k q o -> c (t k q o)"))\
                    .then_inc(s[f"w_in{sl}"], 16)

            def embed(b, k):
                if k % 2 == 0:
                    if k == 0:
                        load_embed_w(b, 0)
                        load_embed_w(b, 1)
                    if k < 14:
                        load_embed_w(b, k + 2)
                        load_embed_w(b, k + 3)
                load_embed_x(b, k)

            def load_max_t(b, h):
                if h >= 2:
                    sp.wait_ge(s["max_done"], 64 * b + 8 * (h - 1))
                sp.dma_start(max_t[h % 2][:, :], d_mt[h]).then_inc(s[f"maxt_in{h % 2}"], 16)

            def load_bias(b, j):
                if j >= 2:
                    sp.wait_ge(s["score_mm"], 64 * b + 16 * (j - 1))
                for hd in range(2):
                    sp.dma_start(bias_t[:, j % 2, hd, :, :].bitcast(f32), d_bt[2 * j + hd]).then_inc(s[f"bias_in{j % 2}"], 16)

            def attention(b, nxt):
                sp.wait_ge(s["split_used"], 32 * b + 32)
                sp.dma_start(w_qkv[:, :, :], a["w_qkvt"].rearrange("(k p) o -> p k o", p=128)).then_inc(s["wqkv_in"], 16)
                sp.dma_start(w_proj[:, :, :], a["w_projt"].rearrange("(k p) o -> p k o", p=128)).then_inc(s["wqkv_in"], 16)
                if positive(128 * b):
                    sp.wait_ge(s["out_done"], 128 * b)
                load_max_t(b, 0)
                load_max_t(b, 1)
                for i in range(4):
                    sp.wait_ge(s["qks_done"], 4 * b + i + 1)
                    stack = q_stack if i < 2 else k_stack
                    parts = (qk_h, qk_h, qk_l) if i < 2 else (qk_h, qk_l, qk_h)
                    for t in range(3):
                        for j in range(4):
                            sp.dma_start(stack[32 * t:32 * t + 32, 4 * (i % 2) + j, :].bitcast(f32),
                                         parts[t][32 * j:32 * j + 32, i, :].bitcast(f32)).then_inc(s["stack_in"], 16)
                sp.wait_ge(s["stack_in"], 768 * b + 768)
                load_bias(b, 0)
                load_bias(b, 1)
                for j in range(4):
                    sp.wait_ge(s["nmax_done"], 4 * b + j + 1)
                    sp.dma_start(q_stack[96:97, 2 * j:2 * j + 2, :].bitcast(f32),
                                 neg_max[:, :].bitcast(f32)).then_inc(s["nmax_in"], 16)
                    if j < 3:
                        load_max_t(b, 2 * j + 2)
                        load_max_t(b, 2 * j + 3)
                    if j in (1, 2):
                        load_bias(b, j + 1)
                    if nxt:
                        for k in range(4 * j, 4 * j + 4):
                            load_stats(b + 1, k)

            def unembed(b):
                load_un_w(b, 0)
                for i in range(8):
                    if i == 0:
                        load_un_w(b, 1)
                        load_un_w(b, 2)
                        load_un_w(b, 3)
                        sp.wait_ge(s["prob_used"], 64 * b + 64)
                        sp.wait_ge(s["max_done"], 64 * b + 64)
                    elif i >= 2:
                        load_un_w(b, 2 * i)
                        load_un_w(b, 2 * i + 1)
                    oh, p = divmod(i, 4)
                    sp.dma_start(x1r[:, oh, p], xv[b, oh * 128:oh * 128 + 128, :, p, :]).then_inc(s[f"xr_in{i}"], 16)

            def store(b, j):
                sp.wait_ge(s["final_done"], 8 * b + j + 1)
                oh, qt = divmod(j, 4)
                sp.dma_start(out[b, oh * 128:oh * 128 + 128, 32 * qt:32 * qt + 32, :],
                             x1[:, oh, 4096 * qt:4096 * qt + 4096].rearrange("c (h w) -> c h w", w=W))\
                    .then_inc(s["out_done"], 16)

            def mlp_weights(b):
                sp.wait_ge(s["rows_mm"], 16 * b + 16)
                sp.dma_start(mlp1[:, :, :], a["w1t"].rearrange("(k p) o -> p k o", p=128)).then_inc(s["mlp_in"], 16)
                sp.dma_start(mlp2[:, :], a["w2t"]).then_inc(s["mlp_in"], 16)

            for k in range(16):
                load_stats(0, k)
            for k in range(16):
                embed(0, k)

            def batch(b, nxt):
                attention(b, nxt)
                unembed(b)
                for k in range(16):
                    if nxt:
                        embed(b + 1, k)
                    if k == 10:
                        mlp_weights(b)
                for j in range(8):
                    store(b, j)

            batches(sp, batch)
            sp.wait_ge(s["out_done"], 128 * B)

        @block.gpsimd
        def _(pool):
            nc.gpsimd.memset(power, -0.5).then_inc(s["power_done"], 1)
            pool.wait_ge(s["power_done"], 1)

            def attention(b, nxt):
                pool.wait_ge(s["split_used"], 32 * b + 32)
                pool.nop().then_inc(s["passed"], 1)
                nc.gpsimd.memset(v[:, :, :, HD:2 * HD], 1.0).then_inc(s["ones_done"], 1)
                pool.wait_ge(s["ones_done"], b + 1)
                if positive(128 * b):
                    pool.wait_ge(s["out_done"], 128 * b)
                    pool.nop().then_inc(s["passed"], 1)
                nc.gpsimd.memset(k_stack[96:97, :, :].bitcast(f32), 1.0).then_inc(s["kone_done"], 1)
                if nxt:
                    rstd_x(b + 1)

            def rstd_x(b):
                pool.wait_ge(s["veps_done"], b + 1)
                nc.gpsimd.tensor_tensor(rstd, veps, power, ALU.pow).then_inc(s["rstd_done"], 1)

            def tail(b):
                pool.wait_ge(s["veps1_done"], b + 1)
                nc.gpsimd.tensor_tensor(rstd1, veps, power, ALU.pow).then_inc(s["rstd1_done"], 1)
                pool.wait_ge(s["gate_done"], b + 1)
                pool.nop().then_inc(s["passed"], 1)
                for j in range(8):
                    oh, qt = divmod(j, 4)
                    part = x1[:, oh, 4096 * qt:4096 * qt + 4096]
                    nc.gpsimd.tensor_scalar(part, part, scale1[:, oh:oh + 1], shift1[:, oh:oh + 1],
                                            ALU.mult, ALU.add).then_inc(s["final_done"], 1)

            rstd_x(0)

            def batch(b, nxt):
                attention(b, nxt)
                tail(b)

            batches(pool, batch)

        @block.scalar
        def _(act):
            act.wait_ge(s["const_in"], 16 * 13)
            nc.scalar.activation(ident[:, :], pro["ident0"][:, :], ACT.Identity).then_inc(s["ident_done"], 1)
            nc.scalar.activation(b_qks[:, 0:2], b_qk[:, 0:2], ACT.Identity, scale=SCALE).then_inc(s["ident_done"], 1)
            nc.scalar.activation(b_qks[:, 2:4], b_qk[:, 2:4], ACT.Identity).then_inc(s["ident_done"], 1)
            for n in range(RAW):
                sl = n % 2
                act.wait_ge(s[f"raw_in{sl}"], raw_in_total(n))
                if n >= 2:
                    act.wait_ge(s[f"raw_out{sl}"], raw_out_total(sl, n - 1))
                w = raw_width(n)
                dst = (pro["raw_h"] if n < RAW_LOW else pro["raw_m"])[:, sl, 0:w]
                nc.scalar.activation(dst, raw_part(n), ACT.Identity).then_inc(s["raw_h_done"], 1)
                if n < 16:
                    for i in range(2):
                        m = 2 * n + i
                        act.wait_ge(s["hid_mm"], m + 1)
                        if m >= 2:
                            act.wait_ge(s["tab_mm"], m - 1)
                        nb = min(512, REL * REL - 512 * (m // 4))
                        nc.scalar.activation(pro["hid"][:, m % 2, 0:nb], PB[m % 2][:, 0:nb], ACT.Relu)\
                            .then_inc(s["hid_done"], 1)

            def normalise(b, k):
                sl, ch = k % 2, k // 8
                if k == 0:
                    act.wait_ge(s["coef_done"], b + 1)
                act.wait_ge(s[f"xs_in{sl}"], 16 * (16 * b + 8 + k // 2 + 1))
                nc.scalar.activation(xs[:, sl, :], xs[:, sl, :], ACT.Identity, bias=shift[:, ch:ch + 1],
                                     scale=rstd[:, ch:ch + 1]).then_inc(s["norm_done"], 1)

            def attention(b):
                for oh in range(2):
                    act.wait_ge(s["split_used"], 32 * b + 32)
                    nc.scalar.activation(z[:, oh, :], PS[oh][:, :], ACT.Identity, bias=b_embed[:, oh:oh + 1])\
                        .then_inc(s["z_done"], 1)
                if positive(128 * b):
                    act.wait_ge(s["out_done"], 128 * b)
                for i in range(4):
                    act.wait_ge(s["qk_mm"], 4 * b + i + 1)
                    nc.scalar.activation(qk[:, i, :], PS[i % 2][:, :], ACT.Identity, bias=b_qks[:, i:i + 1],
                                         scale=SCALE if i < 2 else 1.0).then_inc(s["qk_done"], 1)
                for i in range(2):
                    act.wait_ge(s["v_mm"], 2 * b + i + 1)
                    nc.scalar.activation(v[:, 4 * i:4 * i + 4, :, 0:HD],
                                         PS[i][:, :].rearrange("p (t h d) -> p t h d", t=4, d=HD), ACT.Identity)\
                        .then_inc(s["v_done"], 1)
                for n in range(64):
                    act.wait_ge(s["score_mm"], 64 * b + n + 1)
                    if n >= 2:
                        act.wait_ge(s["prob_used"], 64 * b + n - 1)
                    nc.scalar.activation(prob[:, n % 2, :], PS[n % 2][:, :], ACT.Exp).then_inc(s["exp_done"], 1)
                for oh in range(2):
                    act.wait_ge(s["proj_mm"], 2 * b + oh + 1)
                    nc.scalar.activation(z2[:, 0, oh, :], PS[oh][:, :], ACT.Identity, bias=b_proj[:, oh:oh + 1])\
                        .then_inc(s["z2h_done"], 1)

            def load_rows(b, n):
                oh, cu = divmod(n, 8)
                act.wait_ge(s["x1_done"], 32 * b + 16 * (oh + 1))
                if n == 0:
                    if positive(b):
                        act.wait_ge(s["y2_mm"], b)
                for k in range(16):
                    c = cu + 8 * k
                    act.dma_start(x1t[:, k // 8, k % 8, :], x1[c:c + 1, oh, :].rearrange("c (h w) -> c h w", w=W))\
                        .then_inc(s["rows_in"], 16)

            def unit(b, n):
                act.wait_ge(s["rows_mm"], 16 * b + n + 1)
                if n + 1 < 16 and n != 7:
                    load_rows(b, n + 1)
                if positive(16 * (32 * b + 2 * n)):
                    act.wait_ge(s["sums_in"], 16 * (32 * b + 2 * n))
                nc.scalar.activation(rows[:, :], PB[n % 2][:, :], ACT.Identity).then_inc(s["rows_done"], 1)
                act.wait_ge(s["rows_done"], 16 * b + n + 1)
                oh, cu = divmod(n, 8)
                for u in range(2):
                    act.dma_start(row_sums[cu:cu + 121:8, oh, u, :], rows[u:u + 97:32, :]).then_inc(s["sums_in"], 16)

            def gate_steps(b, step):
                if step == 0:
                    act.wait_ge(s["y1_mm"], b + 1)
                    nc.scalar.activation(hidden, small[0:HID, 16:20], ACT.Relu).then_inc(s["hid1_done"], 1)
                else:
                    act.wait_ge(s["spec_done"], 2 * b + 2)
                    nc.scalar.activation(gexp, gneg, ACT.Exp).then_inc(s["gexp_done"], 1)

            def after(b, nxt):
                load_rows(b, 0)
                for n in range(8):
                    unit(b, n)
                for k in range(16):
                    if nxt:
                        normalise(b + 1, k)
                    if k == 1:
                        load_rows(b, 8)
                    if 2 <= k < 10:
                        unit(b, k + 6)
                    if k == 13:
                        gate_steps(b, 0)
                    if k == 15:
                        gate_steps(b, 1)

            act.wait_ge(s["ident_done"], 3)
            act.wait_ge(s["prep"], 1)
            for k in range(16):
                normalise(0, k)

            def batch(b, nxt):
                attention(b)
                after(b, nxt)

            batches(act, batch)

        @block.vector
        def _(dve):
            def link(ins, name, value):
                ins.then_inc(s[name], 1)
                dve.wait_ge(s[name], value)

            dve.wait_ge(s["const_in"], 16 * 13)
            for n in range(RAW_LOW):
                sl = n % 2
                dve.wait_ge(s["raw_h_done"], n + 1)
                if n >= 2:
                    dve.wait_ge(s[f"raw_out{sl}"], raw_out_total(sl, n - 1))
                w = raw_width(n)
                nc.vector.tensor_tensor(pro["raw_l"][:, sl, 0:w], raw_part(n),
                                        pro["raw_h"][:, sl, 0:w].bitcast(f32), ALU.subtract).then_inc(s["raw_l_done"], 1)
                if n % 2 == 1 and n < 16:
                    m = n // 2
                    dve.wait_ge(s["tab_mm"], 4 * m + 4)
                    nb = min(512, REL * REL - 512 * m)
                    nc.vector.tensor_copy(pro["tab"][:, 512 * m:512 * m + nb], PS[0][0:NH_, 0:nb])\
                        .then_inc(s["tab_done"], 1)
                    if n == 15:
                        dve.wait_ge(s["tab_done"], 8)
                        nc.vector.tensor_copy(pro["tab_rev"][:, :], pro["tab"][:, ::-1]).then_inc(s["rev_done"], 1)
            dve.wait_ge(s["bp_mm"], 1)
            nc.vector.tensor_tensor(b_proj, small[:, 0:2], b_proj, ALU.add).then_inc(s["prep"], 1)

            def stats_sum(b, k):
                sl, ch = k % 2, k // 8
                dve.wait_ge(s[f"xs_in{sl}"], 16 * (16 * b + k // 2 + 1))
                for i in range(4):
                    ins = nc.vector.bn_stats(bn[:, 4 * (k % 8) + i, :], xs[:, sl, 512 * i:512 * i + 512])
                ins.then_inc(s["chunk_done"], 1)
                if k % 8 == 7:
                    dve.wait_ge(s["chunk_done"], 16 * b + k + 1)
                    dve.nop().then_inc(s["passed"], 1)
                    link(nc.vector.bn_aggr(mv[:, ch, :], bn[:, :, :].rearrange("p n t -> p (n t)")),
                         "stat_done", 2 * b + ch + 1)

            def group_dev(b, name, col):
                link(nc.vector.tensor_copy(mean, small[:, col:col + 2]), name, 4 * b + 1)
                link(nc.vector.tensor_tensor(dev, mv[:, :, 0], mean, ALU.subtract), name, 4 * b + 2)
                link(nc.vector.tensor_tensor(var, dev, dev, ALU.mult), name, 4 * b + 3)
                link(nc.vector.tensor_tensor(var, var, mv[:, :, 1], ALU.add), name, 4 * b + 4)

            def group_var(b, mm, done, col):
                dve.wait_ge(s[mm], b + 1)
                nc.vector.tensor_scalar(veps, small[:, col:col + 2], GN_EPS, None, ALU.add).then_inc(s[done], 1)

            def coefficients(b):
                dve.wait_ge(s["gm_mm"], b + 1)
                group_dev(b, "dev_done", 0)
                group_var(b, "gv_mm", "veps_done", 2)
                dve.wait_ge(s["rstd_done"], b + 1)
                nc.vector.scalar_tensor_tensor(shift, mean, -1.0, rstd, ALU.mult, ALU.mult).then_inc(s["coef_done"], 1)

            def split(b, e):
                k, qp = divmod(e, 2)
                sl, hs = k % 2, e % 2
                src = xs[:, sl, :].rearrange("c (t q) -> c q t", q=PT)[:, 2 * qp:2 * qp + 2, :]
                if qp == 0:
                    dve.wait_ge(s["norm_done"], 16 * b + k + 1)
                if e >= 2:
                    dve.wait_ge(s["split_used"], 32 * b + e - 1)
                elif e == 1 and not first(b):
                    dve.wait_ge(s["un_mm"], 32 * b)
                nc.vector.tensor_copy(x_split[:, hs, 0, :, :], src).then_inc(s["h_done"], 1)
                dve.wait_ge(s["h_done"], 32 * b + e + 1)
                nc.vector.tensor_tensor(x_split[:, hs, 1, :, :], src, x_split[:, hs, 0, :, :].bitcast(f32),
                                        ALU.subtract).then_inc(s["split_done"], 1)

            def attention(b, nxt):
                for i in range(4):
                    dve.wait_ge(s["qk_done"], 4 * b + i + 1)
                    link(nc.vector.tensor_copy(qk_h[:, i, :], qk[:, i, :]), "qkh_done", 4 * b + i + 1)
                    nc.vector.tensor_tensor(qk_l[:, i, :], qk[:, i, :], qk_h[:, i, :].bitcast(f32), ALU.subtract)\
                        .then_inc(s["qks_done"], 1)

                def maximum(j, t):
                    hd, nt = divmod(t, 8)
                    h = 2 * j + hd
                    dve.wait_ge(s[f"maxt_in{h % 2}"], 16 * (4 * b + h // 2 + 1))
                    dve.wait_ge(s["smax_mm"], 64 * b + 16 * j + t + 1)
                    off = (HP - 4 - 4 * nt) * WP_
                    if positive(64 * b + 16 * j + t):
                        dve.wait_ge(s["max_done"], 64 * b + 16 * j + t)
                        dve.nop().then_inc(s["passed"], 1)
                    nc.vector.tensor_tensor_reduce(
                        out=dump[:, :], in0=PS[2][:, :], in1=max_t[h % 2][:, off:off + N], scale=1.0, scalar=-3.0e38,
                        op0=ALU.add, op1=ALU.max, accum_out=mx[:, j % 2, t:t + 1]).then_inc(s["max_done"], 1)

                def negate(j):
                    dve.wait_ge(s["tr_mm"], 4 * b + j + 1)
                    if positive(16 * (4 * b + j)):
                        dve.wait_ge(s["nmax_in"], 16 * (4 * b + j))
                    nc.vector.tensor_scalar(neg_max[:, :], PS[2][0:16, 0:128], -1.0, None, ALU.mult)\
                        .then_inc(s["nmax_done"], 1)

                def normalise(j, nh):
                    dve.wait_ge(s["prob_used"], 64 * b + 16 * j + 8 * nh + 8)
                    if positive(8 * b + 2 * j + nh):
                        dve.wait_ge(s["o_done"], 8 * b + 2 * j + nh)
                    link(nc.vector.reciprocal(rows[:, :], PB[nh][:, :]), "recip_done", 8 * b + 2 * j + nh + 1)
                    for hd in range(2):
                        h = 2 * j + hd
                        ins = nc.vector.tensor_tensor(
                            z[32 * (h % 4):32 * (h % 4) + 32, h // 4, 512 * nh:512 * nh + 512],
                            PB[nh][64 * hd:64 * hd + 32, :], rows[64 * hd + 32:64 * hd + 64, :], ALU.mult)
                    ins.then_inc(s["o_done"], 1)

                for t in range(16):
                    maximum(0, t)
                negate(0)
                for j in range(4):
                    done = 0
                    for step in range(16):
                        if j < 3:
                            want = max_tiles(step)
                            while done < want:
                                maximum(j + 1, done)
                                done += 1
                        if step == 2 and j > 0:
                            normalise(j - 1, 1)
                        if step == 10:
                            normalise(j, 0)
                        if j < 3 and step == 13:
                            negate(j + 1)
                        if nxt and step % 4 == 3:
                            stats_sum(b + 1, 4 * j + step // 4)
                normalise(3, 1)
                if nxt:
                    coefficients(b + 1)
                for oh in range(2):
                    dve.wait_ge(s["z2h_done"], 2 * b + oh + 1)
                    nc.vector.scalar_tensor_tensor(z2[:, 1, oh, :], PS[oh][:, :], b_proj[:, oh:oh + 1],
                                                   z2[:, 0, oh, :].bitcast(f32), ALU.add, ALU.subtract)\
                        .then_inc(s["z2_done"], 1)

            def unembed(b):
                for g in range(32):
                    oh, p, q = g // 16, g // 4 % 4, g % 4
                    if q == 0:
                        dve.wait_ge(s[f"xr_in{g // 4}"], 16 * (b + 1))
                    dve.wait_ge(s["un_mm"], 32 * b + g + 1)
                    at = x1v[:, oh, p, q]
                    nc.vector.scalar_tensor_tensor(at, PS[g % 2][:, :].rearrange("c (h w) -> c h w", w=WP_),
                                                   b_un[:, oh:oh + 1], at, ALU.add, ALU.add).then_inc(s["x1_done"], 1)
                    if q == 3:
                        dve.wait_ge(s["x1_done"], 32 * b + g + 1)
                        for i in range(8):
                            ins = nc.vector.bn_stats(bn[:, 8 * p + i, :], x1r[:, oh, p, 4 * i:4 * i + 4, :])
                        ins.then_inc(s["bn_done"], 1)
                        dve.wait_ge(s["bn_done"], 8 * b + g // 4 + 1)
                        dve.nop().then_inc(s["passed"], 1)
                        if p == 3:
                            link(nc.vector.bn_aggr(mv[:, oh, :], bn[:, :, :].rearrange("p n t -> p (n t)")),
                                 "mv1_done", 2 * b + oh + 1)

            def gate_part(b, step):
                if step == 0:
                    dve.wait_ge(s["gm1_mm"], b + 1)
                    group_dev(b, "dev1_done", 4)
                elif step == 1:
                    group_var(b, "gv1_mm", "veps1_done", 6)
                elif step == 2:
                    dve.wait_ge(s["sums_in"], 16 * 32 * (b + 1))
                    dve.wait_ge(s["rstd1_done"], b + 1)
                    for n in range(8):
                        oh, f = divmod(n, 4)
                        u, vv = divmod(f, 2)
                        link(nc.vector.tensor_tensor_reduce(
                            out=rows[:, 0:W], in0=row_sums[:, oh, u, :], in1=cos_w[:, vv, :], scale=1.0, scalar=0.0,
                            op0=ALU.mult, op1=ALU.add, accum_out=spec[:, oh, f:f + 1]), "spec_link", 12 * b + n + 1)
                    for f in range(4):
                        link(nc.vector.scalar_tensor_tensor(spec[:, :, f], mean, -plane_sums[f], spec[:, :, f],
                                                            ALU.mult, ALU.add), "spec_link", 12 * b + 9 + f)
                    for oh in range(2):
                        ins = nc.vector.tensor_scalar(spec[:, oh, :], spec[:, oh, :], rstd1[:, oh:oh + 1], None, ALU.mult)
                    ins.then_inc(s["spec_done"], 1)
                elif step == 3:
                    dve.wait_ge(s["y2_mm"], b + 1)
                    link(nc.vector.tensor_reduce(gsum, small[:, 24:32].rearrange("p (o f) -> p o f", f=4), AX.X, ALU.add),
                         "gate_link", 5 * b + 1)
                    nc.vector.tensor_scalar(gneg, gsum, -0.25, 80.0, ALU.mult, ALU.min).then_inc(s["spec_done"], 1)
                else:
                    dve.wait_ge(s["gexp_done"], b + 1)
                    link(nc.vector.tensor_scalar(gexp, gexp, 1.0, None, ALU.add), "gate_link", 5 * b + 2)
                    link(nc.vector.reciprocal(gate, gexp), "gate_link", 5 * b + 3)
                    link(nc.vector.tensor_tensor(gr, gate, rstd1, ALU.mult), "gate_link", 5 * b + 4)
                    link(nc.vector.tensor_scalar(scale1, gr, 1.0, None, ALU.add), "gate_link", 5 * b + 5)
                    nc.vector.scalar_tensor_tensor(shift1, mean, -1.0, gr, ALU.mult, ALU.mult).then_inc(s["gate_done"], 1)

            def after(b, nxt):
                for k in range(16):
                    if nxt:
                        split(b + 1, 2 * k)
                        split(b + 1, 2 * k + 1)
                    for step in {1: (0,), 3: (1,), 11: (2,), 15: (3, 4)}.get(k, ()):
                        gate_part(b, step)

            for k in range(16):
                stats_sum(0, k)
            coefficients(0)
            for e in range(32):
                split(0, e)

            def batch(b, nxt):
                attention(b, nxt)
                unembed(b)
                after(b, nxt)

            batches(dve, batch)

        @block.tensor
        def _(pe):
            pe.wait_ge(s["const_in"], 16 * 13)
            pe.wait_ge(s["wqkv_in"], 16)
            pe.wait_ge(s["ident_done"], 1)
            for n in range(16):
                for i in range(2):
                    m = 2 * n + i
                    cb, kt = divmod(m, 4)
                    nb = min(512, REL * REL - 512 * cb)
                    if positive(m - 1):
                        pe.wait_ge(s["hid_done"], m - 1)
                    nc.tensor.matmul(PB[m % 2][:, 0:nb], pro["cpb1"][:, 128 * kt:128 * kt + 128],
                                     pro["rel"][:, 512 * cb:512 * cb + nb], start=True, stop=True).then_inc(s["hid_mm"], 1)
                    pe.wait_ge(s["hid_done"], m + 1)
                    if kt == 0:
                        if positive(cb):
                            pe.wait_ge(s["tab_done"], cb)
                    nc.tensor.matmul(PS[0][0:NH_, 0:nb], pro["cpb2"][:, kt, :], pro["hid"][:, m % 2, 0:nb],
                                     start=kt == 0, stop=kt == 3).then_inc(s["tab_mm"], 1)
            for oh in range(2):
                for ch in range(2):
                    ins = nc.tensor.matmul(small[:, oh:oh + 1], w_proj[:, ch, 128 * oh:128 * oh + 128], b_v[:, ch:ch + 1],
                                           start=ch == 0, stop=ch == 1)
            ins.then_inc(s["bp_mm"], 1)

            def tiny(after_, value, rhs, col, done):
                pe.wait_ge(s[after_], value)
                nc.tensor.matmul(small[:, col:col + 2], group[:, :], rhs, start=True, stop=True).then_inc(s[done], 1)

            def embed_sub(b, e):
                k, qp = divmod(e, 2)
                i, nh = divmod(k, 2)
                w = 2 * i + qp
                pe.wait_ge(s["split_done"], 32 * b + e + 1)
                pe.wait_ge(s[f"w_in{w % 4}"], 16 * (8 * b + w // 4 + 1))
                if e == 0 and not first(b):
                    pe.wait_ge(s["x1_done"], 32 * b)
                if e == 0 and first(b):
                    pe.wait_ge(s["tab_done"], 8)
                wr = w_ring[:, w % 4, :].rearrange("c (t q o) -> c t q o", t=2, o=C)
                for q in range(2):
                    for oh in range(2):
                        for t, (wt, xt) in enumerate(((0, 0), (0, 1), (1, 0))):
                            ins = nc.tensor.matmul(PS[oh][:, 512 * nh:512 * nh + 512], wr[:, wt, q, 128 * oh:128 * oh + 128],
                                                   x_split[:, e % 2, xt, q, :],
                                                   start=(i == 0 and qp == 0 and q == 0 and t == 0),
                                                   stop=(i == 7 and qp == 1 and q == 1 and t == 2))
                ins.then_inc(s["split_used"], 1)

            def attention(b, nxt):
                pe.wait_ge(s["z_done"], 2 * b + 2)
                pe.wait_ge(s["wqkv_in"], 32 * b + 48)
                for i in range(4):
                    if i >= 2:
                        pe.wait_ge(s["qk_done"], 4 * b + i - 1)
                    col = 128 * i
                    for nh in range(2):
                        for ch in range(2):
                            ins = nc.tensor.matmul(PS[i % 2][:, 512 * nh:512 * nh + 512], w_qkv[:, ch, col:col + 128],
                                                   z[:, ch, 512 * nh:512 * nh + 512], start=ch == 0, stop=ch == 1)
                    ins.then_inc(s["qk_mm"], 1)
                for i in range(2):
                    pe.wait_ge(s["qk_done"], 4 * b + 3 + i)
                    for t in range(4):
                        mt = 4 * i + t
                        for ch in range(2):
                            ins = nc.tensor.matmul(PS[i][:, 256 * t:256 * t + 256], z[:, ch, 128 * mt:128 * mt + 128],
                                                   w_qkv[:, ch, 512:768], start=ch == 0 , stop=ch == 1)
                    ins.then_inc(s["v_mm"], 1)

                def score_max(j, t):
                    hd, nt = divmod(t, 8)
                    h = 2 * j + hd
                    if positive(64 * b + 16 * j + t):
                        pe.wait_ge(s["max_done"], 64 * b + 16 * j + t)
                    for mh in range(2):
                        ins = nc.tensor.matmul(PS[2][:, 512 * mh:512 * mh + 512], q_stack[0:96, h, 128 * nt:128 * nt + 128],
                                               k_stack[0:96, h, 512 * mh:512 * mh + 512], start=True, stop=True)
                    ins.then_inc(s["smax_mm"], 1)

                def transpose_max(j):
                    pe.wait_ge(s["max_done"], 64 * b + 16 * j + 16)
                    nc.tensor.transpose(PS[2][0:16, 0:128], mx[:, j % 2, :], ident[:, :].bitcast(f32)).then_inc(s["tr_mm"], 1)

                def scores(j, step):
                    nh, mt = divmod(step, 8)
                    n = 16 * j + step
                    if n >= 2:
                        pe.wait_ge(s["exp_done"], 64 * b + n - 1)
                    else:
                        pe.wait_ge(s["v_done"], 2 * b + 2)
                    off = (HP - 4 - 4 * mt) * WP_ + 512 * nh
                    for hd in range(2):
                        h = 2 * j + hd
                        at = PS[n % 2][:, 512 * hd:512 * hd + 512]
                        nc.tensor.matmul(at, k_stack[0:97, h, 128 * mt:128 * mt + 128],
                                         q_stack[0:97, h, 512 * nh:512 * nh + 512], start=True, stop=False)
                        for t in range(2):
                            ins = nc.tensor.matmul(at, ident[:, :], bias_t[:, j % 2, hd, t, off:off + 512],
                                                   start=False, stop=t == 1)
                    ins.then_inc(s["score_mm"], 1)

                def values(j, step):
                    nh, mt = divmod(step, 8)
                    n = 16 * j + step
                    pe.wait_ge(s["exp_done"], 64 * b + n + 1)
                    if mt == 0 and n >= 16:
                        pe.wait_ge(s["o_done"], 8 * b + 2 * (j - 1) + nh + 1)
                    for hd in range(2):
                        ins = nc.tensor.matmul(PB[nh][64 * hd:64 * hd + 64, :], v[:, mt, 2 * j + hd, :],
                                               prob[:, n % 2, 512 * hd:512 * hd + 512], start=mt == 0, stop=mt == 7)
                    ins.then_inc(s["prob_used"], 1)

                pe.wait_ge(s["stack_in"], 768 * b + 768)
                for t in range(16):
                    score_max(0, t)
                transpose_max(0)
                pe.wait_ge(s["kone_done"], b + 1)
                pe.wait_ge(s["ones_done"], b + 1)
                for j in range(4):
                    pe.wait_ge(s[f"bias_in{j % 2}"], 32 * (2 * b + j // 2 + 1))
                    pe.wait_ge(s["nmax_in"], 16 * (4 * b + j + 1))
                    done = 0
                    for step in range(16):
                        scores(j, step)
                        if j < 3:
                            want = max_tiles(step)
                            if done == 0:
                                pe.wait_ge(s["nmax_done"], 4 * b + j + 1)
                            while done < want:
                                score_max(j + 1, done)
                                done += 1
                        if step or j:
                            values(*divmod(16 * j + step - 1, 16))
                        if j < 3 and step == 13:
                            transpose_max(j + 1)
                values(3, 15)
                if nxt:
                    pe.wait_ge(s["nmax_done"], 4 * b + 4)
                    tiny("stat_done", 2 * b + 4, mv[:, :, 0], 0, "gm_mm")
                    tiny("dev_done", 4 * b + 8, var, 2, "gv_mm")
                pe.wait_ge(s["o_done"], 8 * b + 8)
                for oh in range(2):
                    for nh in range(2):
                        for ch in range(2):
                            ins = nc.tensor.matmul(PS[oh][:, 512 * nh:512 * nh + 512], w_proj[:, ch, 128 * oh:128 * oh + 128],
                                                   z[:, ch, 512 * nh:512 * nh + 512], start=ch == 0, stop=ch == 1)
                    ins.then_inc(s["proj_mm"], 1)

            def un_group(b, g):
                oh, p, q = g // 16, g // 4 % 4, g % 4
                w = 2 * (g // 4) + q // 2
                sl = (w + 3) % 4
                if g < 2:
                    pe.wait_ge(s["z2_done"], 2 * b + 2)
                else:
                    pe.wait_ge(s["x1_done"], 32 * b + g - 1)
                pe.wait_ge(s[f"w_in{sl}"], 16 * (8 * b + 4 + w // 4 + 1))
                wr = w_ring[:, sl, :].rearrange("c (t k q o) -> c t k q o", t=2, k=2, q=2)
                for nh in range(2):
                    for ch in range(2):
                        for t, (wt, zt) in enumerate(((0, 0), (0, 1), (1, 0))):
                            ins = nc.tensor.matmul(PS[g % 2][:, 512 * nh:512 * nh + 512], wr[:, wt, ch, q % 2, :],
                                                   z2[:, zt, ch, 512 * nh:512 * nh + 512],
                                                   start=ch == 0 and t == 0, stop=ch == 1 and t == 2)
                ins.then_inc(s["un_mm"], 1)

            def unit(b, n):
                pe.wait_ge(s["rows_in"], 256 * (16 * b + n + 1))
                if n >= 2:
                    pe.wait_ge(s["rows_done"], 16 * b + n - 1)
                for j in range(2):
                    for i in range(2):
                        t = 2 * j + i
                        ins = nc.tensor.matmul(PB[n % 2][32 * t:32 * t + 32, :], cos_h[:, :],
                                               x1t[:, j, 4 * i:4 * i + 4, :].rearrange("h c w -> h (c w)"),
                                               start=True, stop=True)
                ins.then_inc(s["rows_mm"], 1)

            def gate_mm(b, step):
                if step == 0:
                    tiny("mv1_done", 2 * b + 2, mv[:, :, 0], 4, "gm1_mm")
                elif step == 1:
                    tiny("dev1_done", 4 * b + 4, var, 6, "gv1_mm")
                elif step == 2:
                    pe.wait_ge(s["spec_done"], 2 * b + 1)
                    pe.wait_ge(s["mlp_in"], 32 * b + 32)
                    for ch in range(2):
                        ins = nc.tensor.matmul(small[0:HID, 16:20], mlp1[:, ch, :], spec[:, ch, :], start=ch == 0, stop=ch == 1)
                    ins.then_inc(s["y1_mm"], 1)
                else:
                    pe.wait_ge(s["hid1_done"], b + 1)
                    for oh in range(2):
                        ins = nc.tensor.matmul(small[:, 24 + 4 * oh:28 + 4 * oh], mlp2[:, 128 * oh:128 * oh + 128], hidden,
                                               start=True, stop=True)
                    ins.then_inc(s["y2_mm"], 1)

            def after(b, nxt):
                for g in range(32):
                    un_group(b, g)
                    if g >= 18 and g % 2 == 0 and (g - 18) // 2 < 7:
                        unit(b, (g - 18) // 2)
                unit(b, 7)
                for k in range(16):
                    if nxt:
                        embed_sub(b + 1, 2 * k)
                        embed_sub(b + 1, 2 * k + 1)
                    if 1 <= k < 9:
                        unit(b, k + 7)
                    for step in {0: (0,), 2: (1,), 12: (2,), 14: (3,)}.get(k, ()):
                        gate_mm(b, step)

            pe.wait_ge(s["prep"], 1)
            tiny("stat_done", 2, mv[:, :, 0], 0, "gm_mm")
            tiny("dev_done", 4, var, 2, "gv_mm")
            for e in range(32):
                embed_sub(0, e)

            def batch(b, nxt):
                attention(b, nxt)
                after(b, nxt)

            batches(pe, batch)


def kernel(**inputs):
    import math
    import numpy as np
    import concourse.bacc as bacc
    from concourse.bass_utils import run_bass_kernel_spmd

    def dct_rows(n):
        i = np.arange(n, dtype=np.float32)[:, None]
        j = np.arange(n, dtype=np.float32)[None, :]
        m = np.cos(math.pi * j * (2.0 * i + 1.0) / (2.0 * n)) * math.sqrt(2.0 / n)
        m[0] *= math.sqrt(0.5)
        return m[0:2].astype(np.float32)

    g = {k: np.asarray(v) for k, v in inputs.items()}
    c = np.ascontiguousarray

    def columns(vec):
        return c(vec.reshape(-1, 128).T)

    ah, aw = dct_rows(H), dct_rows(W)
    cos_h = np.zeros((H, 32), np.float32)
    cos_h[:, 0:2] = ah.T
    r = (np.arange(REL, dtype=np.float32) - np.float32(HP - 1)) / np.float32(HP - 1)
    rel = np.stack([np.repeat(r, REL), np.tile(r, REL), np.ones(REL * REL, np.float32)])
    arrays = {
        "x": g["x"],
        "w_embed": c(g["L0_conv_w_embed"].transpose(1, 2, 3, 0)).reshape(C, PT, PT * C),
        "w_unembed": c(g["L0_conv_w_unembed"].transpose(0, 2, 3, 1)).reshape(C, PT, PT * C),
        "w_qkvt": c(g["L0_conv_w_qkv"].T), "w_projt": c(g["L0_conv_w_proj"].T),
        "b_embed": columns(g["L0_conv_b_embed"]), "b_unembed": columns(g["L0_conv_b_unembed"]),
        "b_proj": columns(g["L0_conv_b_proj"]), "b_v": columns(g["L0_conv_b_qkv"][2 * C:]),
        "b_qk": columns(g["L0_conv_b_qkv"][:2 * C]),
        "cpb_w1t": c(g["L0_conv_cpb_w1"].T), "cpb_b1": g["L0_conv_cpb_b1"].reshape(1, CPB),
        "cpb_w2t": c(g["L0_conv_cpb_w2"].T),
        "w1t": c(g["L1_conv_w1"].T), "w2t": c(g["L1_conv_w2"].T),
        "identity": np.eye(128, dtype=np.float32),
        "group_mean": np.kron(np.eye(16, dtype=np.float32), np.full((8, 8), 0.125, np.float32)),
        "cos_h": cos_h, "cos_w": c(np.broadcast_to(aw[None], (128, 2, W))), "rel": rel,
    }
    sums = [float(ah[u].astype(np.float64).sum() * aw[w].astype(np.float64).sum()) for u in range(2) for w in range(2)]
    nc = bacc.Bacc("TRN2", target_bir_lowering=False, num_devices=1)
    aps = {k: nc.dram_tensor("in_" + k, v.shape, mybir.dt.from_np(v.dtype), kind="ExternalInput").ap()
           for k, v in arrays.items()}
    aps["out"] = nc.dram_tensor("x_out", (B, C, H, W), mybir.dt.float32, kind="ExternalOutput").ap()
    build(nc, aps, sums)
    res = run_bass_kernel_spmd(nc, [{"in_" + k: v for k, v in arrays.items()}], core_ids=[0])
    return res.results[0]["x_out"]
```

```python
import concourse.bass as bass
from concourse import mybir
from contextlib import ExitStack

B, C, H, W = 8, 256, 128, 128
PT = 4
HP, WP_ = H // PT, W // PT
N = HP * WP_
NH_, HD = 8, 32
HID = C // 4
CPB = 512
REL = 2 * HP - 1
UB = (2 * HP - PT) * WP_
GN_EPS = 1e-5


def build(nc, a, plane_sums):
    f32, f32r, bf16 = mybir.dt.float32, mybir.dt.float32r, mybir.dt.bfloat16
    ALU, ACT = mybir.AluOpType, mybir.ActivationFunctionType
    AX = mybir.AxisListType
    SCALE = float(HD) ** -0.5

    d_we = nc.dram_tensor("split_embed", [8, 2, 128, 2, 512], f32, kind="Internal").ap()
    d_wu = nc.dram_tensor("split_unembed", [2, 4, 2, 128, 2, 2, 2, 128], f32, kind="Internal").ap()
    d_tab = nc.dram_tensor("bias_table", [2, NH_, REL * REL], f32, kind="Internal").ap()
    d_bt = nc.dram_tensor("bias_split", [NH_, 128, 2, UB], f32, kind="Internal").ap()
    d_mt = nc.dram_tensor("bias_for_max", [NH_, 128, UB], bf16, kind="Internal").ap()

    x, out = a["x"], a["out"]
    xv = x.rearrange("b c (hp p) w -> b c hp p w", p=PT)

    ctx = ExitStack()
    with ctx:
        def region(*layouts):
            seen, most = {}, 0
            for layout in layouts:
                with ExitStack() as piece:
                    size = 0
                    for name, shape, dt in layout:
                        seen[name] = piece.enter_context(nc.sbuf_tensor(name, shape, dt))
                        k = 2 if dt == bf16 else 4
                        for s in shape[1:]:
                            k *= s
                        size += (k + 31) // 32 * 32
                    most = max(most, size)
            ctx.enter_context(nc.sbuf_tensor("hold_" + layouts[0][0][0], [128, most // 4], f32))
            return seen

        r = region(
            [("x1", [128, 2, H * W], f32)],
            [("bias_t", [128, 2, 2, 2, UB], f32r), ("max_t0", [128, UB], bf16),
             ("q_stack", [128, NH_, N], f32r), ("k_stack", [128, NH_, N], f32r)],
            [("pair0_bias", [128, 2, 2, UB], f32), ("qk", [128, 4, N], f32)],
            [("raw", [128, 2, UB], f32), ("raw_h", [128, 2, UB], f32r), ("raw_l", [128, 2, UB], f32r),
             ("rel", [3, REL * REL], f32), ("hid", [128, 2, 512], f32), ("tab", [NH_, REL * REL], f32),
             ("tab_rev", [NH_, REL * REL], f32), ("cpb1", [3, CPB], f32), ("cpb2", [128, 4, NH_], f32),
             ("raw_m", [128, 2, UB], bf16), ("ident0", [128, 128], f32)])
        x1, bias_t, q_stack, k_stack = r["x1"], r["bias_t"], r["q_stack"], r["k_stack"]
        qk = r["qk"]
        pro = r
        x1v = x1[:, :, :].rearrange("c o (hp p wp q) -> c o p q hp wp", p=PT, wp=WP_, q=PT)
        x1r = x1[:, :, :].rearrange("c o (hp p w) -> c o p hp w", p=PT, w=W)
        xs = region([("x_stream", [128, 2, 2048], f32)])["x_stream"]
        r = region([("x_rows", [128, 2, 8, W], f32)],
                   [("basis", [128, 8, 4 * PT * PT], f32), ("mlp1", [128, 2, HID], f32), ("mlp2", [HID, C], f32),
                    ("zf", [128, 2, PT * PT, 2, 4], f32r)])
        x_rows, basis, mlp1, mlp2, zf = r["x_rows"], r["basis"], r["mlp1"], r["mlp2"], r["zf"]
        r = region([("x_split", [128, 2, 2, 2, 512], f32r)],
                   [("prob", [128, 2, 1024], f32), ("v", [128, 8, NH_, 2 * HD], f32)],
                   [("pad", [128, 2048], f32), ("z2", [128, 2, 2, N], f32r)])
        x_split, prob, v, z2 = r["x_split"], r["prob"], r["v"], r["z2"]
        r = region([("w_ring", [128, 4, 1024], f32r)],
                   [("w_qkv", [128, 2, 3 * C], f32), ("dump", [128, N], bf16), ("w_proj", [128, 2, C], f32),
                    ("max_t1", [128, UB], bf16), ("unit_rows", [128, 512], f32)])
        w_ring, w_qkv, w_proj, dump, unit_rows = r["w_ring"], r["w_qkv"], r["w_proj"], r["dump"], r["unit_rows"]
        max_t = [pro["max_t0"], r["max_t1"]]
        r = region([("z", [128, 2, N], f32)], [("z2t", [128, 8, C], f32)], [("x_third", [128, 2048], f32)])
        z, z2t = r["z"], r["z2t"]
        xbuf = [xs[:, 0, :], xs[:, 1, :], r["x_third"][:, :]]

        def sb(name, shape, dt=f32):
            return ctx.enter_context(nc.sbuf_tensor(name, shape, dt))

        rows = sb("rows", [128, 512])
        row_sums = sb("row_sums", [128, 2, 2, W])
        ident = sb("ident", [128, 128], f32r)
        group = sb("group", [128, 128])
        cos_w = sb("cos_w", [128, 2, W])
        cos_h = sb("cos_h", [128, 32])
        bn = sb("bn", [128, 32, 6])
        neg_max = sb("neg_max", [16, 128], f32r)
        mx = sb("mx", [128, 2, 16])
        vec = sb("vec", [128, 64])
        b_embed, b_un, b_proj, b_v = (vec[:, 2 * i:2 * i + 2] for i in range(4))
        b_qk = vec[:, 8:12]
        b_qks = vec[:, 12:16]
        mv = vec[:, 16:20].rearrange("p (c t) -> p c t", t=2)
        dev, var, veps, power = (vec[:, 20 + 2 * i:22 + 2 * i] for i in range(4))
        rstd, shift = vec[:, 28:30], vec[:, 30:32]
        spec = vec[:, 32:40].rearrange("p (o f) -> p o f", f=4)
        gsum, gexp, gate, gr = (vec[:, 40 + 2 * i:42 + 2 * i] for i in range(4))
        scale1, shift1 = vec[:, 48:50], vec[:, 50:52]
        hidden = vec[0:HID, 52:56]
        rstd1, negm1 = vec[:, 56:58], vec[:, 58:60]
        mean, gneg = vec[:, 60:62], vec[:, 62:64]

        PS = [ctx.enter_context(nc.psum_tensor(f"wide{i}", [128, 1024], f32)) for i in range(3)]
        PB = [ctx.enter_context(nc.psum_tensor(f"bank{i}", [128, 512], f32)) for i in range(2)]
        small = PS[2]

        def sem(name):
            return ctx.enter_context(nc.semaphore(name))

        s = {}
        for name in (
            "const_in raw_in0 raw_in1 raw_out0 raw_out1 tab_out xs_in0 xs_in1 xs_in2 w_in0 w_in1 w_in2 w_in3 "
            "wqkv_in stack_in0 stack_in1 bias_in0 bias_in1 maxt_in0 maxt_in1 nmax_in "
            "xr_in0 xr_in1 xr_in2 xr_in3 xr_in4 xr_in5 xr_in6 xr_in7 rows_in0 rows_in1 sums_in gate_in out_done "
            "ident_done raw_h_done raw_l_done hid_mm hid_done tab_mm tab_done rev_done bp_mm prep "
            "split_used qk_mm v_mm smax_mm tr_mm score_mm prob_used proj_mm un_mm rows_mm z2t_mm zf_mm wu_used "
            "gm_mm gv_mm gm1_mm gv1_mm y1_mm y2_mm "
            "norm_done z_done qk_done high_done v_done exp_done z2h_done rows_done z2t_done zfh_done hid1_done gexp_done "
            "h_done split_done low_done max_done nmax_done recip_done o_done z2_done x1_done bn_done "
            "chunk_done stat_done dev_done veps_done coef_done mv1_done dev1_done veps1_done spec_link spec_done zf_done gate_link gate_done "
            "ones_done kone_done power_done rstd_done rstd1_done final_done passed"
        ).split():
            s[name] = sem(name)

        block = ctx.enter_context(nc.Block())

        def positive(count):
            return not isinstance(count, int) or count > 0

        def max_tiles(step):
            return min(16, (16 * (step + 1) + 12) // 13)

        RAW = 8 + 8 + NH_ + NH_
        RAW_LOW = 8 + 8 + NH_

        def first(b):
            return isinstance(b, int) and b == 0

        def batches(eng, step):
            step(0, True)
            with eng.Fori(1, B - 1) as b:
                step(b, True)
            step(B - 1, False)

        def raw_in_total(n):
            return 16 * sum(1 if m < 16 else 4 if m < RAW_LOW else 4 for m in range(n % 2, n + 1, 2))

        def raw_out_total(sl, count):
            return 16 * sum(2 if m < 8 else 8 if m < 16 else 2 if m < RAW_LOW else 1 for m in range(sl, count, 2))

        def raw_width(n):
            return 1024 if n < 16 else UB

        XS_IN = (8 + 6, 8 + 5, 5)

        def chunk_loads(b, k):
            return 16 * (XS_IN[k % 3] * b + (8 if k % 3 < 2 else 0) + k // 3 + 1)

        UNIT_STEPS = (4, 7, 12, 15)

        def unit_bank(n):
            return PB[1 - n % 4 // 2]

        HALF = (0, 2, 1, 3)

        def max_bank(j, t):
            return PS[2] if j else PS[(2, 1, 0)[t % 3]]

        def raw_part(n):
            part = pro["raw"][:, n % 2, 0:raw_width(n)]
            return part if n < 16 else part[:, ::-1]

        @block.sync
        def _(sp):
            def const(dst, src):
                sp.dma_start(dst, src).then_inc(s["const_in"], 16)

            const(pro["ident0"][:, :], a["identity"])
            const(group[:, :], a["group_mean"])
            const(cos_w[:, :, :], a["cos_w"])
            const(cos_h[:, :], a["cos_h"])
            const(pro["rel"][:, :], a["rel"])
            const(pro["cpb1"][0:2, :], a["cpb_w1t"])
            const(pro["cpb1"][2:3, :], a["cpb_b1"])
            const(pro["cpb2"][:, :, :], a["cpb_w2t"].rearrange("(t p) h -> p t h", p=128))
            const(b_embed, a["b_embed"])
            const(b_un, a["b_unembed"])
            const(b_proj, a["b_proj"])
            const(b_v, a["b_v"])
            const(b_qk, a["b_qk"])
            sp.dma_start(w_proj[:, :, :], a["w_projt"].rearrange("(k p) o -> p k o", p=128)).then_inc(s["wqkv_in"], 16)

            def raw_load(n):
                sl = n % 2
                inc = s[f"raw_in{sl}"]
                if n >= 2:
                    sp.wait_ge(s["raw_h_done"], n - 1)
                    sp.wait_ge(s["raw_l_done"], min(n - 1, RAW_LOW))
                raw = pro["raw"][:, sl, :]
                if n < 16:
                    w = a["w_embed"] if n < 8 else a["w_unembed"]
                    ch, p = divmod(n % 8, 4)
                    sp.dma_start(raw[:, 0:1024], w[ch * 128:ch * 128 + 128, p, :]).then_inc(inc, 16)
                    return
                if n == 16:
                    sp.wait_ge(s["tab_out"], 32)
                t, h = divmod(n - 16, NH_)
                for i in range(4):
                    src = bass.AP(d_tab.tensor, ((1 - t) * NH_ + h) * REL * REL + i * REL,
                                  [[1, 32], [REL, UB // WP_], [1, WP_]])
                    sp.dma_start(raw[32 * i:32 * i + 32, :].rearrange("p (r c) -> p r c", c=WP_), src)\
                        .then_inc(inc, 16)

            def raw_store(n):
                sl = n % 2
                inc = s[f"raw_out{sl}"]
                sp.wait_ge(s["raw_h_done"], n + 1)
                if n < RAW_LOW:
                    sp.wait_ge(s["raw_l_done"], n + 1)
                hl = (pro["raw_h"][:, sl, :].bitcast(f32), pro["raw_l"][:, sl, :].bitcast(f32))
                ch, p = divmod(n % 8, 4)
                for t in range(2):
                    if n < 8:
                        sp.dma_start(d_we[n].rearrange("q c t w -> t c q w")[t],
                                     hl[t][:, 0:1024].rearrange("c (q w) -> c q w", q=2)).then_inc(inc, 16)
                    elif n < 16:
                        src = hl[t][:, 0:1024].rearrange("c (q o k) -> c q o k", o=2, k=128)
                        for oh in range(2):
                            for qp in range(2):
                                sp.dma_start(d_wu[oh, p, qp, :, t, ch, :, :], src[:, 2 * qp:2 * qp + 2, oh, :])\
                                    .then_inc(inc, 16)
                    elif n < RAW_LOW:
                        sp.dma_start(d_bt[n - 16, :, t, :], hl[t]).then_inc(inc, 16)
                    elif t == 0:
                        sp.dma_start(d_mt[n - RAW_LOW], pro["raw_m"][:, sl, :]).then_inc(inc, 16)

            raw_load(0)
            for n in range(RAW):
                if n == 15:
                    sp.wait_ge(s["tab_done"], 8)
                    sp.dma_start(d_tab[0], pro["tab"][:, :]).then_inc(s["tab_out"], 16)
                    sp.wait_ge(s["rev_done"], 1)
                    sp.dma_start(d_tab[1], pro["tab_rev"][:, :]).then_inc(s["tab_out"], 16)
                if n + 1 < RAW:
                    raw_load(n + 1)
                raw_store(n)
            for sl in range(2):
                sp.wait_ge(s[f"raw_out{sl}"], raw_out_total(sl, RAW))


            def load_stats(b, k):
                if k >= 2:
                    sp.wait_ge(s["chunk_done"], 16 * b + k - 1)
                elif not first(b):
                    sp.wait_ge(s["split_done"], 32 * (b - 1) + 2 * (15, 13)[k] + 2)
                ch, kk = divmod(k, 8)
                src = x[b, ch * 128:ch * 128 + 128, kk * 16:kk * 16 + 16, :]
                sp.dma_start(xbuf[k % 2].rearrange("c (h w) -> c h w", w=W), src).then_inc(s[f"xs_in{k % 2}"], 16)

            def load_embed_x(b, k):
                if k >= 3:
                    sp.wait_ge(s["split_done"], 32 * b + 2 * (k - 3) + 2)
                elif k < 2:
                    sp.wait_ge(s["chunk_done"], 16 * b + 15 + k)
                elif not first(b):
                    sp.wait_ge(s["zf_mm"], b)
                (ch, p), nh = divmod(k // 2, 4), k % 2
                src = xv[b, ch * 128:ch * 128 + 128, nh * 16:nh * 16 + 16, p, :]
                sp.dma_start(xbuf[k % 3].rearrange("c (h w) -> c h w", w=W), src).then_inc(s[f"xs_in{k % 3}"], 16)

            def load_embed_w(b, w):
                i, qp = divmod(w, 2)
                if w >= 4:
                    sp.wait_ge(s["split_used"], 32 * b + 4 * (i - 2) + 3 + qp)
                elif not first(b):
                    sp.wait_ge(s["wu_used"], 32 * (b - 1) + 2 * (12 + w) + 2)
                else:
                    sp.wait_ge(s["bp_mm"], 1)
                sp.dma_start(w_ring[:, w % 4, :].bitcast(f32), d_we[i, qp].rearrange("c t w -> c (t w)"))\
                    .then_inc(s[f"w_in{w % 4}"], 16)

            def load_un_w(b, w):
                if w >= 4:
                    sp.wait_ge(s["wu_used"], 32 * b + 2 * (w - 4) + 2)
                elif w == 0:
                    sp.wait_ge(s["v_mm"], 2 * b + 2)
                elif w == 1:
                    sp.wait_ge(s["max_done"], 64 * b + 64)
                elif w == 2:
                    sp.wait_ge(s["proj_mm"], 2 * b + 2)
                else:
                    sp.wait_ge(s["sums_in"], 16 * (32 * b + 32))
                (oh, p), qp = divmod(w // 2, 4), w % 2
                sp.dma_start(w_ring[:, w % 4, :].bitcast(f32), d_wu[oh, p, qp].rearrange("c t k q o -> c (t k q o)"))\
                    .then_inc(s[f"w_in{w % 4}"], 16)

            def load_unit(b, n):
                if n == 0:
                    if positive(b):
                        sp.wait_ge(s["y2_mm"], b)
                for j in range(2):
                    if n > 0:
                        sp.wait_ge(s["rows_mm"], 32 * b + 2 * n + j - 1)
                    c0 = 16 * n + 8 * j
                    sp.dma_start(x_rows[:, j, :, :], x[b, c0:c0 + 8, :, :].rearrange("c h w -> h c w"))\
                        .then_inc(s[f"rows_in{j}"], 16)

            def embed(b, k):
                if k == 0:
                    for w in range(4):
                        load_embed_w(b, w)
                load_embed_x(b, k)
                if k % 2 and k >= 5:
                    load_embed_w(b, k - 1)
                    load_embed_w(b, k)

            def load_max_t(b, h):
                if h >= 2:
                    sp.wait_ge(s["max_done"], 64 * b + 8 * (h - 1))
                sp.dma_start(max_t[h % 2][:, :], d_mt[h]).then_inc(s[f"maxt_in{h % 2}"], 16)

            def load_bias(b, j):
                if j >= 2:
                    sp.wait_ge(s["score_mm"], 64 * b + 16 * (j - 1))
                for hd in range(2):
                    sp.dma_start(bias_t[:, j % 2, hd, :, :].bitcast(f32), d_bt[2 * j + hd]).then_inc(s[f"bias_in{j % 2}"], 16)

            def attention(b, nxt):
                sp.wait_ge(s["split_used"], 32 * b + 32)
                sp.dma_start(w_qkv[:, :, :], a["w_qkvt"].rearrange("(k p) o -> p k o", p=128)).then_inc(s["wqkv_in"], 16)
                sp.dma_start(w_proj[:, :, :], a["w_projt"].rearrange("(k p) o -> p k o", p=128)).then_inc(s["wqkv_in"], 16)
                if positive(128 * b):
                    sp.wait_ge(s["out_done"], 128 * b)
                load_max_t(b, 0)
                load_max_t(b, 1)
                for n in range(4):
                    sp.wait_ge(s["high_done"], 16 * b + 4 * n + 4)
                    i = HALF[n]
                    stack, to = (q_stack, 32) if i < 2 else (k_stack, 64)
                    heads = slice(4 * (i % 2), 4 * (i % 2) + 4)
                    sp.dma_start(stack[to:to + 32, heads, :].bitcast(f32), stack[0:32, heads, :].bitcast(f32))\
                        .then_inc(s[f"stack_in{n // 2}"], 16)
                    if n == 1:
                        load_bias(b, 0)
                        load_unit(b, 0)
                sp.wait_ge(s["low_done"], 16 * b + 16)
                load_bias(b, 1)
                for j in range(4):
                    if j < 3:
                        load_max_t(b, 2 * j + 2)
                        load_max_t(b, 2 * j + 3)
                    if j in (1, 2):
                        load_bias(b, j + 1)
                    if nxt:
                        load_stats(b + 1, 4 * j)
                        load_stats(b + 1, 4 * j + 1)
                    load_unit(b, 4 * j + 1)
                    if nxt:
                        load_stats(b + 1, 4 * j + 2)
                        load_stats(b + 1, 4 * j + 3)
                    if j == 3:
                        load_un_w(b, 0)
                    for n in range(4 * j + 2, min(4 * j + 5, 16)):
                        load_unit(b, n)

            def unembed(b):
                sp.wait_ge(s["rows_mm"], 32 * b + 32)
                sp.dma_start(basis[:, :, :], a["basis"]).then_inc(s["gate_in"], 16)
                sp.dma_start(mlp1[:, :, :], a["w1t"].rearrange("(k p) o -> p k o", p=128)).then_inc(s["gate_in"], 16)
                sp.dma_start(mlp2[:, :], a["w2t"]).then_inc(s["gate_in"], 16)
                def load_x(i):
                    oh, p = divmod(i, 4)
                    sp.dma_start(x1r[:, oh, p], xv[b, oh * 128:oh * 128 + 128, :, p, :]).then_inc(s[f"xr_in{i}"], 16)

                load_un_w(b, 1)
                sp.wait_ge(s["prob_used"], 64 * b + 64)
                sp.wait_ge(s["max_done"], 64 * b + 64)
                load_x(0)
                load_un_w(b, 3)
                load_un_w(b, 2)
                load_x(1)
                load_x(2)
                for i in range(2, 8):
                    load_un_w(b, 2 * i)
                    if i + 1 < 8:
                        load_x(i + 1)
                    load_un_w(b, 2 * i + 1)

            def store(b, j):
                sp.wait_ge(s["final_done"], 8 * b + j + 1)
                oh, qt = divmod(j, 4)
                sp.dma_start(out[b, oh * 128:oh * 128 + 128, 32 * qt:32 * qt + 32, :],
                             x1[:, oh, 4096 * qt:4096 * qt + 4096].rearrange("c (h w) -> c h w", w=W))\
                    .then_inc(s["out_done"], 16)

            for k in range(16):
                load_stats(0, k)
            for k in range(16):
                embed(0, k)

            def batch(b, nxt):
                attention(b, nxt)
                unembed(b)
                for k in range(16):
                    if nxt:
                        embed(b + 1, k)
                    if k >= 9:
                        store(b, k - 9)
                for j in range(7, 8):
                    store(b, j)

            batches(sp, batch)
            sp.wait_ge(s["out_done"], 128 * B)

        @block.gpsimd
        def _(pool):
            nc.gpsimd.memset(power, -0.5).then_inc(s["power_done"], 1)
            pool.wait_ge(s["power_done"], 1)

            def attention(b, nxt):
                pool.wait_ge(s["split_used"], 32 * b + 32)
                pool.nop().then_inc(s["passed"], 1)
                nc.gpsimd.memset(v[:, :, :, HD:2 * HD], 1.0).then_inc(s["ones_done"], 1)
                pool.wait_ge(s["ones_done"], b + 1)
                if positive(128 * b):
                    pool.wait_ge(s["out_done"], 128 * b)
                    pool.nop().then_inc(s["passed"], 1)
                nc.gpsimd.memset(k_stack[96:97, :, :].bitcast(f32), 1.0).then_inc(s["kone_done"], 1)
                if nxt:
                    rstd_x(b + 1)

            def rstd_x(b):
                pool.wait_ge(s["veps_done"], b + 1)
                nc.gpsimd.tensor_tensor(rstd, veps, power, ALU.pow).then_inc(s["rstd_done"], 1)

            def tail(b):
                pool.wait_ge(s["veps1_done"], b + 1)
                nc.gpsimd.tensor_tensor(rstd1, veps, power, ALU.pow).then_inc(s["rstd1_done"], 1)
                pool.wait_ge(s["gate_done"], b + 1)
                pool.nop().then_inc(s["passed"], 1)
                for j in range(8):
                    oh, qt = divmod(j, 4)
                    part = x1[:, oh, 4096 * qt:4096 * qt + 4096]
                    nc.gpsimd.tensor_scalar(part, part, scale1[:, oh:oh + 1], shift1[:, oh:oh + 1],
                                            ALU.mult, ALU.add).then_inc(s["final_done"], 1)

            rstd_x(0)

            def batch(b, nxt):
                attention(b, nxt)
                tail(b)

            batches(pool, batch)

        @block.scalar
        def _(act):
            act.wait_ge(s["const_in"], 16 * 13)
            nc.scalar.activation(ident[:, :], pro["ident0"][:, :], ACT.Identity).then_inc(s["ident_done"], 1)
            nc.scalar.activation(b_qks[:, 0:2], b_qk[:, 0:2], ACT.Identity, scale=SCALE).then_inc(s["ident_done"], 1)
            nc.scalar.activation(b_qks[:, 2:4], b_qk[:, 2:4], ACT.Identity).then_inc(s["ident_done"], 1)
            for n in range(RAW):
                sl = n % 2
                act.wait_ge(s[f"raw_in{sl}"], raw_in_total(n))
                if n >= 2:
                    act.wait_ge(s[f"raw_out{sl}"], raw_out_total(sl, n - 1))
                w = raw_width(n)
                dst = (pro["raw_h"] if n < RAW_LOW else pro["raw_m"])[:, sl, 0:w]
                nc.scalar.activation(dst, raw_part(n), ACT.Identity).then_inc(s["raw_h_done"], 1)
                if n < 16:
                    for i in range(2):
                        m = 2 * n + i
                        act.wait_ge(s["hid_mm"], m + 1)
                        if m >= 2:
                            act.wait_ge(s["tab_mm"], m - 1)
                        nb = min(512, REL * REL - 512 * (m // 4))
                        nc.scalar.activation(pro["hid"][:, m % 2, 0:nb], PB[m % 2][:, 0:nb], ACT.Relu)\
                            .then_inc(s["hid_done"], 1)

            def normalise(b, k):
                sl, ch = k % 3, k // 8
                if k == 0:
                    act.wait_ge(s["coef_done"], b + 1)
                act.wait_ge(s[f"xs_in{sl}"], chunk_loads(b, k))
                nc.scalar.activation(xbuf[sl], xbuf[sl], ACT.Identity, bias=shift[:, ch:ch + 1],
                                     scale=rstd[:, ch:ch + 1]).then_inc(s["norm_done"], 1)

            def move_max(b, j):
                act.wait_ge(s["nmax_done"], 4 * b + j + 1)
                act.dma_start(q_stack[96:97, 2 * j:2 * j + 2, :].bitcast(f32),
                              neg_max[:, :].bitcast(f32)).then_inc(s["nmax_in"], 16)

            def attention(b):
                for oh in range(2):
                    act.wait_ge(s["split_used"], 32 * b + 32)
                    nc.scalar.activation(z[:, oh, :], PS[oh][:, :], ACT.Identity, bias=b_embed[:, oh:oh + 1])\
                        .then_inc(s["z_done"], 1)
                if positive(128 * b):
                    act.wait_ge(s["out_done"], 128 * b)
                for n in range(4):
                    i = HALF[n]
                    act.wait_ge(s["qk_mm"], 4 * b + n + 1)
                    nc.scalar.activation(qk[:, i, :], PS[n % 2][:, :], ACT.Identity, bias=b_qks[:, i:i + 1],
                                         scale=SCALE if i < 2 else 1.0).then_inc(s["qk_done"], 1)
                    act.wait_ge(s["qk_done"], 4 * b + n + 1)
                    stack = q_stack if i < 2 else k_stack
                    for k in range(4):
                        nc.scalar.activation(stack[0:32, 4 * (i % 2) + k, :], qk[32 * k:32 * k + 32, i, :], ACT.Identity)\
                            .then_inc(s["high_done"], 1)
                for i in range(2):
                    act.wait_ge(s["v_mm"], 2 * b + i + 1)
                    nc.scalar.activation(v[:, 4 * i:4 * i + 4, :, 0:HD],
                                         PS[i][:, :].rearrange("p (t h d) -> p t h d", t=4, d=HD), ACT.Identity)\
                        .then_inc(s["v_done"], 1)
                move_max(b, 0)
                for n in range(64):
                    act.wait_ge(s["score_mm"], 64 * b + n + 1)
                    if n >= 2:
                        act.wait_ge(s["prob_used"], 64 * b + n - 1)
                    nc.scalar.activation(prob[:, n % 2, :], PS[n % 2][:, :], ACT.Exp).then_inc(s["exp_done"], 1)
                    if n % 16 == 13 and n < 48:
                        move_max(b, n // 16 + 1)
                    if n % 16 in UNIT_STEPS:
                        unit_out(b, 4 * (n // 16) + UNIT_STEPS.index(n % 16))
                for oh in range(2):
                    act.wait_ge(s["proj_mm"], 2 * b + oh + 1)
                    nc.scalar.activation(z2[:, 0, oh, :], PS[oh][:, :], ACT.Identity, bias=b_proj[:, oh:oh + 1])\
                        .then_inc(s["z2h_done"], 1)

            def unit_out(b, n):
                act.wait_ge(s["rows_mm"], 2 * (16 * b + n) + 2)
                if n > 0:
                    act.wait_ge(s["sums_in"], 16 * (32 * b + 2 * n))
                elif positive(b):
                    act.wait_ge(s["spec_done"], 2 * b)
                nc.scalar.activation(unit_rows[:, :], unit_bank(n)[:, :], ACT.Identity).then_inc(s["rows_done"], 1)
                act.wait_ge(s["rows_done"], 16 * b + n + 1)
                oh, cu = divmod(16 * n, 128)
                for u in range(2):
                    act.dma_start(row_sums[cu:cu + 16, oh, u, :], unit_rows[u:u + 97:32, :]).then_inc(s["sums_in"], 16)

            def z2_turned(b):
                for i, src in enumerate((PS[2][:, :], PB[0][:, :], PB[1][:, :])):
                    act.wait_ge(s["z2t_mm"], 3 * b + i + 1)
                    t0 = (0, 4, 6)[i]
                    t1 = (4, 6, 8)[i]
                    nc.scalar.activation(z2t[:, t0:t1, :].rearrange("p t k -> p (t k)"), src, ACT.Identity)\
                        .then_inc(s["z2t_done"], 1)
                act.wait_ge(s["zf_mm"], b + 1)
                nc.scalar.activation(zf[:, :, :, 0, :], PB[1][:, 0:128].rearrange("p (k g f) -> p k g f", k=2, f=4), ACT.Identity)\
                    .then_inc(s["zfh_done"], 1)

            def gate_steps(b, step):
                if step == 0:
                    act.wait_ge(s["y1_mm"], b + 1)
                    nc.scalar.activation(hidden, small[0:HID, 16:20], ACT.Relu).then_inc(s["hid1_done"], 1)
                else:
                    act.wait_ge(s["spec_done"], 2 * b + 2)
                    nc.scalar.activation(gexp, gneg, ACT.Exp).then_inc(s["gexp_done"], 1)

            def after(b, nxt):
                z2_turned(b)
                for k in range(16):
                    if nxt:
                        normalise(b + 1, k)
                    if k == 5:
                        gate_steps(b, 0)
                    if k == 7:
                        gate_steps(b, 1)

            act.wait_ge(s["ident_done"], 3)
            act.wait_ge(s["prep"], 1)
            for k in range(16):
                normalise(0, k)

            def batch(b, nxt):
                attention(b)
                after(b, nxt)

            batches(act, batch)

        @block.vector
        def _(dve):
            def link(ins, name, value):
                ins.then_inc(s[name], 1)
                dve.wait_ge(s[name], value)

            dve.wait_ge(s["const_in"], 16 * 13)
            for n in range(RAW_LOW):
                sl = n % 2
                dve.wait_ge(s["raw_h_done"], n + 1)
                if n >= 2:
                    dve.wait_ge(s[f"raw_out{sl}"], raw_out_total(sl, n - 1))
                w = raw_width(n)
                nc.vector.tensor_tensor(pro["raw_l"][:, sl, 0:w], raw_part(n),
                                        pro["raw_h"][:, sl, 0:w].bitcast(f32), ALU.subtract).then_inc(s["raw_l_done"], 1)
                if n % 2 == 1 and n < 16:
                    m = n // 2
                    dve.wait_ge(s["tab_mm"], 4 * m + 4)
                    nb = min(512, REL * REL - 512 * m)
                    nc.vector.tensor_copy(pro["tab"][:, 512 * m:512 * m + nb], PS[0][0:NH_, 0:nb])\
                        .then_inc(s["tab_done"], 1)
                    if n == 15:
                        dve.wait_ge(s["tab_done"], 8)
                        nc.vector.tensor_copy(pro["tab_rev"][:, :], pro["tab"][:, ::-1]).then_inc(s["rev_done"], 1)
            dve.wait_ge(s["bp_mm"], 1)
            nc.vector.tensor_tensor(b_proj, small[:, 0:2], b_proj, ALU.add).then_inc(s["prep"], 1)

            def stats_sum(b, k):
                sl, ch = k % 2, k // 8
                dve.wait_ge(s[f"xs_in{sl}"], 16 * (XS_IN[sl] * b + k // 2 + 1))
                for i in range(4):
                    ins = nc.vector.bn_stats(bn[:, 4 * (k % 8) + i, :], xs[:, sl, 512 * i:512 * i + 512])
                ins.then_inc(s["chunk_done"], 1)
                if k % 8 == 7:
                    dve.wait_ge(s["chunk_done"], 16 * b + k + 1)
                    dve.nop().then_inc(s["passed"], 1)
                    link(nc.vector.bn_aggr(mv[:, ch, :], bn[:, :, :].rearrange("p n t -> p (n t)")),
                         "stat_done", 2 * b + ch + 1)

            def group_dev(b, name, col):
                link(nc.vector.tensor_copy(mean, small[:, col:col + 2]), name, 4 * b + 1)
                link(nc.vector.tensor_tensor(dev, mv[:, :, 0], mean, ALU.subtract), name, 4 * b + 2)
                link(nc.vector.tensor_tensor(var, dev, dev, ALU.mult), name, 4 * b + 3)
                link(nc.vector.tensor_tensor(var, var, mv[:, :, 1], ALU.add), name, 4 * b + 4)

            def group_var(b, mm, done, col):
                dve.wait_ge(s[mm], b + 1)
                nc.vector.tensor_scalar(veps, small[:, col:col + 2], GN_EPS, None, ALU.add).then_inc(s[done], 1)

            def coefficients(b):
                dve.wait_ge(s["gm_mm"], b + 1)
                group_dev(b, "dev_done", 0)
                group_var(b, "gv_mm", "veps_done", 2)
                dve.wait_ge(s["rstd_done"], b + 1)
                nc.vector.scalar_tensor_tensor(shift, mean, -1.0, rstd, ALU.mult, ALU.mult).then_inc(s["coef_done"], 1)

            def split(b, e):
                k, qp = divmod(e, 2)
                hs = e % 2
                src = xbuf[k % 3].rearrange("c (t q) -> c q t", q=PT)[:, 2 * qp:2 * qp + 2, :]
                if qp == 0:
                    dve.wait_ge(s["norm_done"], 16 * b + k + 1)
                if e >= 2:
                    dve.wait_ge(s["split_used"], 32 * b + e - 1)
                elif e == 1 and not first(b):
                    dve.wait_ge(s["un_mm"], 32 * b)
                nc.vector.tensor_copy(x_split[:, hs, 0, :, :], src).then_inc(s["h_done"], 1)
                dve.wait_ge(s["h_done"], 32 * b + e + 1)
                nc.vector.tensor_tensor(x_split[:, hs, 1, :, :], src, x_split[:, hs, 0, :, :].bitcast(f32),
                                        ALU.subtract).then_inc(s["split_done"], 1)

            def attention(b, nxt):
                def low_parts(n):
                    i = HALF[n]
                    stack, to = (q_stack, 64) if i < 2 else (k_stack, 32)
                    for k in range(4):
                        h = 4 * (i % 2) + k
                        dve.wait_ge(s["high_done"], 16 * b + 4 * n + k + 1)
                        nc.vector.tensor_tensor(stack[to:to + 32, h, :], qk[32 * k:32 * k + 32, i, :],
                                                stack[0:32, h, :].bitcast(f32), ALU.subtract).then_inc(s["low_done"], 1)

                def maximum(j, t):
                    hd, nt = divmod(t, 8)
                    h = 2 * j + hd
                    dve.wait_ge(s[f"maxt_in{h % 2}"], 16 * (4 * b + h // 2 + 1))
                    dve.wait_ge(s["smax_mm"], 64 * b + 16 * j + t + 1)
                    off = (HP - 4 - 4 * nt) * WP_
                    if positive(64 * b + 16 * j + t):
                        dve.wait_ge(s["max_done"], 64 * b + 16 * j + t)
                        dve.nop().then_inc(s["passed"], 1)
                    nc.vector.tensor_tensor_reduce(
                        out=dump[:, :], in0=max_bank(j, t)[:, :], in1=max_t[h % 2][:, off:off + N], scale=1.0, scalar=-3.0e38,
                        op0=ALU.add, op1=ALU.max, accum_out=mx[:, j % 2, t:t + 1]).then_inc(s["max_done"], 1)

                def negate(j):
                    dve.wait_ge(s["tr_mm"], 4 * b + j + 1)
                    if positive(16 * (4 * b + j)):
                        dve.wait_ge(s["nmax_in"], 16 * (4 * b + j))
                    nc.vector.tensor_scalar(neg_max[:, :], PS[2][0:16, 0:128], -1.0, None, ALU.mult)\
                        .then_inc(s["nmax_done"], 1)

                def normalise(j, nh):
                    dve.wait_ge(s["prob_used"], 64 * b + 16 * j + 8 * nh + 8)
                    if positive(8 * b + 2 * j + nh):
                        dve.wait_ge(s["o_done"], 8 * b + 2 * j + nh)
                    link(nc.vector.reciprocal(rows[:, :], PB[nh][:, :]), "recip_done", 8 * b + 2 * j + nh + 1)
                    for hd in range(2):
                        h = 2 * j + hd
                        ins = nc.vector.tensor_tensor(
                            z[32 * (h % 4):32 * (h % 4) + 32, h // 4, 512 * nh:512 * nh + 512],
                            PB[nh][64 * hd:64 * hd + 32, :], rows[64 * hd + 32:64 * hd + 64, :], ALU.mult)
                    ins.then_inc(s["o_done"], 1)

                low_parts(0)
                low_parts(1)
                for t in range(16):
                    maximum(0, t)
                negate(0)
                low_parts(2)
                low_parts(3)
                for j in range(4):
                    done = 0
                    for step in range(16):
                        if j < 3:
                            want = max_tiles(step)
                            while done < want:
                                maximum(j + 1, done)
                                done += 1
                        if step == 2 and j > 0:
                            normalise(j - 1, 1)
                        if step == 10:
                            normalise(j, 0)
                        if j < 3 and step == 13:
                            negate(j + 1)
                        if nxt and step in (2, 5, 8, 11):
                            stats_sum(b + 1, 4 * j + step // 3)
                normalise(3, 1)
                if nxt:
                    coefficients(b + 1)
                for oh in range(2):
                    dve.wait_ge(s["z2h_done"], 2 * b + oh + 1)
                    nc.vector.scalar_tensor_tensor(z2[:, 1, oh, :], PS[oh][:, :], b_proj[:, oh:oh + 1],
                                                   z2[:, 0, oh, :].bitcast(f32), ALU.add, ALU.subtract)\
                        .then_inc(s["z2_done"], 1)

            def unembed(b):
                def x1_stats(g):
                    oh, p, q = g // 16, g // 4 % 4, g % 4
                    if q == 0:
                        dve.wait_ge(s["x1_done"], 32 * b + g + 4)
                    for i in range(2 * q, 2 * q + 2):
                        ins = nc.vector.bn_stats(bn[:, 8 * p + i, :], x1r[:, oh, p, 4 * i:4 * i + 4, :])
                    ins.then_inc(s["bn_done"], 1)
                    if g % 16 == 15:
                        dve.wait_ge(s["bn_done"], 32 * b + g + 1)
                        dve.nop().then_inc(s["passed"], 1)
                        link(nc.vector.bn_aggr(mv[:, oh, :], bn[:, :, :].rearrange("p n t -> p (n t)")),
                             "mv1_done", 2 * b + oh + 1)

                for g in range(32):
                    oh, p, q = g // 16, g // 4 % 4, g % 4
                    if q == 0:
                        dve.wait_ge(s[f"xr_in{g // 4}"], 16 * (b + 1))
                    dve.wait_ge(s["un_mm"], 32 * b + g + 1)
                    at = x1v[:, oh, p, q]
                    nc.vector.scalar_tensor_tensor(at, PS[g % 2][:, :].rearrange("c (h w) -> c h w", w=WP_),
                                                   b_un[:, oh:oh + 1], at, ALU.add, ALU.add).then_inc(s["x1_done"], 1)
                    if g == 1:
                        dve.wait_ge(s["zfh_done"], b + 1)
                        nc.vector.tensor_tensor(zf[:, :, :, 1, :], PB[1][:, 0:128].rearrange("p (k g f) -> p k g f", k=2, f=4),
                                                zf[:, :, :, 0, :].bitcast(f32), ALU.subtract).then_inc(s["zf_done"], 1)
                    if g >= 4:
                        x1_stats(g - 4)
                for g in range(28, 32):
                    x1_stats(g)

            def gate_part(b, step):
                if step == 0:
                    dve.wait_ge(s["gm1_mm"], b + 1)
                    group_dev(b, "dev1_done", 4)
                elif step == 1:
                    group_var(b, "gv1_mm", "veps1_done", 6)
                elif step == 5:
                    dve.wait_ge(s["sums_in"], 16 * 32 * (b + 1))
                    for n in range(8):
                        oh, f = divmod(n, 4)
                        u, vv = divmod(f, 2)
                        link(nc.vector.tensor_tensor_reduce(
                            out=rows[:, 0:W], in0=row_sums[:, oh, u, :], in1=cos_w[:, vv, :], scale=1.0, scalar=0.0,
                            op0=ALU.mult, op1=ALU.add, accum_out=spec[:, oh, f:f + 1]), "spec_link", 15 * b + n + 1)
                elif step == 2:
                    dve.wait_ge(s["wu_used"], 32 * b + 32)
                    y_of = PB[0][:, 0:16].rearrange("p (o t f) -> p o t f", t=2, f=4)
                    for t in range(2):
                        link(nc.vector.tensor_tensor(spec, y_of[:, :, t, :], spec, ALU.add), "spec_link", 15 * b + 9 + t)
                    link(nc.vector.tensor_tensor(gneg, b_un, mean, ALU.subtract), "spec_link", 15 * b + 11)
                    for f in range(4):
                        link(nc.vector.scalar_tensor_tensor(spec[:, :, f], gneg, plane_sums[f], spec[:, :, f],
                                                            ALU.mult, ALU.add), "spec_link", 15 * b + 12 + f)
                    dve.wait_ge(s["rstd1_done"], b + 1)
                    for oh in range(2):
                        ins = nc.vector.tensor_scalar(spec[:, oh, :], spec[:, oh, :], rstd1[:, oh:oh + 1], None, ALU.mult)
                    ins.then_inc(s["spec_done"], 1)
                elif step == 3:
                    dve.wait_ge(s["y2_mm"], b + 1)
                    link(nc.vector.tensor_reduce(gsum, small[:, 24:32].rearrange("p (o f) -> p o f", f=4), AX.X, ALU.add),
                         "gate_link", 5 * b + 1)
                    nc.vector.tensor_scalar(gneg, gsum, -0.25, 80.0, ALU.mult, ALU.min).then_inc(s["spec_done"], 1)
                else:
                    dve.wait_ge(s["gexp_done"], b + 1)
                    link(nc.vector.tensor_scalar(gexp, gexp, 1.0, None, ALU.add), "gate_link", 5 * b + 2)
                    link(nc.vector.reciprocal(gate, gexp), "gate_link", 5 * b + 3)
                    link(nc.vector.tensor_tensor(gr, gate, rstd1, ALU.mult), "gate_link", 5 * b + 4)
                    link(nc.vector.tensor_scalar(scale1, gr, 1.0, None, ALU.add), "gate_link", 5 * b + 5)
                    nc.vector.scalar_tensor_tensor(shift1, mean, -1.0, gr, ALU.mult, ALU.mult).then_inc(s["gate_done"], 1)

            def after(b, nxt):
                for k in range(16):
                    if nxt:
                        split(b + 1, 2 * k)
                        split(b + 1, 2 * k + 1)
                    for step in {0: (5,), 1: (0,), 2: (1,), 3: (2,), 5: (3,), 6: (4,)}.get(k, ()):
                        gate_part(b, step)

            for k in range(16):
                stats_sum(0, k)
            coefficients(0)
            for e in range(32):
                split(0, e)

            def batch(b, nxt):
                attention(b, nxt)
                unembed(b)
                after(b, nxt)

            batches(dve, batch)

        @block.tensor
        def _(pe):
            pe.wait_ge(s["const_in"], 16 * 13)
            pe.wait_ge(s["wqkv_in"], 16)
            pe.wait_ge(s["ident_done"], 1)
            for n in range(16):
                for i in range(2):
                    m = 2 * n + i
                    cb, kt = divmod(m, 4)
                    nb = min(512, REL * REL - 512 * cb)
                    if positive(m - 1):
                        pe.wait_ge(s["hid_done"], m - 1)
                    nc.tensor.matmul(PB[m % 2][:, 0:nb], pro["cpb1"][:, 128 * kt:128 * kt + 128],
                                     pro["rel"][:, 512 * cb:512 * cb + nb], start=True, stop=True).then_inc(s["hid_mm"], 1)
                    pe.wait_ge(s["hid_done"], m + 1)
                    if kt == 0:
                        if positive(cb):
                            pe.wait_ge(s["tab_done"], cb)
                    nc.tensor.matmul(PS[0][0:NH_, 0:nb], pro["cpb2"][:, kt, :], pro["hid"][:, m % 2, 0:nb],
                                     start=kt == 0, stop=kt == 3).then_inc(s["tab_mm"], 1)
            for oh in range(2):
                for ch in range(2):
                    ins = nc.tensor.matmul(small[:, oh:oh + 1], w_proj[:, ch, 128 * oh:128 * oh + 128], b_v[:, ch:ch + 1],
                                           start=ch == 0, stop=ch == 1)
            ins.then_inc(s["bp_mm"], 1)

            def tiny(after_, value, rhs, col, done):
                pe.wait_ge(s[after_], value)
                nc.tensor.matmul(small[:, col:col + 2], group[:, :], rhs, start=True, stop=True).then_inc(s[done], 1)

            def embed_sub(b, e):
                k, qp = divmod(e, 2)
                i, nh = divmod(k, 2)
                w = 2 * i + qp
                pe.wait_ge(s["split_done"], 32 * b + e + 1)
                pe.wait_ge(s[f"w_in{w % 4}"], 16 * (8 * b + w // 4 + 1))
                if e == 0 and not first(b):
                    pe.wait_ge(s["x1_done"], 32 * b)
                if e == 0 and first(b):
                    pe.wait_ge(s["tab_done"], 8)
                wr = w_ring[:, w % 4, :].rearrange("c (t q o) -> c t q o", t=2, o=C)
                for q in range(2):
                    for oh in range(2):
                        for t, (wt, xt) in enumerate(((0, 0), (0, 1), (1, 0))):
                            ins = nc.tensor.matmul(PS[oh][:, 512 * nh:512 * nh + 512], wr[:, wt, q, 128 * oh:128 * oh + 128],
                                                   x_split[:, e % 2, xt, q, :],
                                                   start=(i == 0 and qp == 0 and q == 0 and t == 0),
                                                   stop=(i == 7 and qp == 1 and q == 1 and t == 2))
                ins.then_inc(s["split_used"], 1)

            def attention(b, nxt):
                pe.wait_ge(s["z_done"], 2 * b + 2)
                pe.wait_ge(s["wqkv_in"], 32 * b + 48)
                for n in range(4):
                    if n >= 2:
                        pe.wait_ge(s["qk_done"], 4 * b + n - 1)
                    i, col = n, 128 * HALF[n]
                    for nh in range(2):
                        for ch in range(2):
                            ins = nc.tensor.matmul(PS[i % 2][:, 512 * nh:512 * nh + 512], w_qkv[:, ch, col:col + 128],
                                                   z[:, ch, 512 * nh:512 * nh + 512], start=ch == 0, stop=ch == 1)
                    ins.then_inc(s["qk_mm"], 1)
                for i in range(2):
                    pe.wait_ge(s["qk_done"], 4 * b + 3 + i)
                    for t in range(4):
                        mt = 4 * i + t
                        for ch in range(2):
                            ins = nc.tensor.matmul(PS[i][:, 256 * t:256 * t + 256], z[:, ch, 128 * mt:128 * mt + 128],
                                                   w_qkv[:, ch, 512:768], start=ch == 0 , stop=ch == 1)
                    ins.then_inc(s["v_mm"], 1)

                def score_max(j, t):
                    hd, nt = divmod(t, 8)
                    h = 2 * j + hd
                    if j > 0:
                        pe.wait_ge(s["max_done"], 64 * b + 16 * j + t)
                    elif t >= 3:
                        pe.wait_ge(s["max_done"], 64 * b + t - 2)
                    elif t >= 1:
                        pe.wait_ge(s["v_done"], 2 * b + 3 - t)
                    elif positive(b):
                        pe.wait_ge(s["spec_done"], 2 * b)
                    for mh in range(2):
                        ins = nc.tensor.matmul(max_bank(j, t)[:, 512 * mh:512 * mh + 512], q_stack[0:96, h, 128 * nt:128 * nt + 128],
                                               k_stack[0:96, h, 512 * mh:512 * mh + 512], start=True, stop=True)
                    ins.then_inc(s["smax_mm"], 1)

                def transpose_max(j):
                    pe.wait_ge(s["max_done"], 64 * b + 16 * j + 16)
                    nc.tensor.transpose(PS[2][0:16, 0:128], mx[:, j % 2, :], ident[:, :].bitcast(f32)).then_inc(s["tr_mm"], 1)

                def scores(j, step):
                    nh, mt = divmod(step, 8)
                    n = 16 * j + step
                    if n >= 2:
                        pe.wait_ge(s["exp_done"], 64 * b + n - 1)
                    else:
                        pe.wait_ge(s["v_done"], 2 * b + 2)
                    off = (HP - 4 - 4 * mt) * WP_ + 512 * nh
                    for hd in range(2):
                        h = 2 * j + hd
                        at = PS[n % 2][:, 512 * hd:512 * hd + 512]
                        nc.tensor.matmul(at, k_stack[0:97, h, 128 * mt:128 * mt + 128],
                                         q_stack[0:97, h, 512 * nh:512 * nh + 512], start=True, stop=False)
                        for t in range(2):
                            ins = nc.tensor.matmul(at, ident[:, :], bias_t[:, j % 2, hd, t, off:off + 512],
                                                   start=False, stop=t == 1)
                    ins.then_inc(s["score_mm"], 1)

                def values(j, step):
                    nh, mt = divmod(step, 8)
                    n = 16 * j + step
                    pe.wait_ge(s["exp_done"], 64 * b + n + 1)
                    if mt == 0 and n >= 16:
                        pe.wait_ge(s["o_done"], 8 * b + 2 * (j - 1) + nh + 1)
                    if mt == 0 and (nh or j):
                        pe.wait_ge(s["rows_done"], 16 * b + 4 * j + 2 * nh)
                    for hd in range(2):
                        ins = nc.tensor.matmul(PB[nh][64 * hd:64 * hd + 64, :], v[:, mt, 2 * j + hd, :],
                                               prob[:, n % 2, 512 * hd:512 * hd + 512], start=mt == 0, stop=mt == 7)
                    ins.then_inc(s["prob_used"], 1)

                pe.wait_ge(s["stack_in0"], 32 * b + 32)
                pe.wait_ge(s["low_done"], 16 * b + 8)
                for t in range(16):
                    score_max(0, t)
                transpose_max(0)
                pe.wait_ge(s["kone_done"], b + 1)
                pe.wait_ge(s["ones_done"], b + 1)
                for j in range(4):
                    pe.wait_ge(s[f"bias_in{j % 2}"], 32 * (2 * b + j // 2 + 1))
                    pe.wait_ge(s["nmax_in"], 16 * (4 * b + j + 1))
                    done = 0
                    for step in range(16):
                        scores(j, step)
                        if j < 3:
                            want = max_tiles(step)
                            if done == 0:
                                pe.wait_ge(s["nmax_done"], 4 * b + j + 1)
                            if done == 0 and j == 1:
                                pe.wait_ge(s["stack_in1"], 32 * b + 32)
                                pe.wait_ge(s["low_done"], 16 * b + 16)
                            if done < want:
                                score_max(j + 1, done)
                                done += 1
                        if step or j:
                            values(*divmod(16 * j + step - 1, 16))
                        if j < 3 and done < want:
                            score_max(j + 1, done)
                            done += 1
                        if j < 3 and step == 13:
                            transpose_max(j + 1)
                        if step in UNIT_STEPS:
                            unit(b, 4 * j + UNIT_STEPS.index(step))
                values(3, 15)
                if nxt:
                    pe.wait_ge(s["nmax_done"], 4 * b + 4)
                    tiny("stat_done", 2 * b + 4, mv[:, :, 0], 0, "gm_mm")
                    tiny("dev_done", 4 * b + 8, var, 2, "gv_mm")
                pe.wait_ge(s["o_done"], 8 * b + 8)
                for oh in range(2):
                    for nh in range(2):
                        for ch in range(2):
                            ins = nc.tensor.matmul(PS[oh][:, 512 * nh:512 * nh + 512], w_proj[:, ch, 128 * oh:128 * oh + 128],
                                                   z[:, ch, 512 * nh:512 * nh + 512], start=ch == 0, stop=ch == 1)
                    ins.then_inc(s["proj_mm"], 1)

            def un_group(b, g):
                oh, p, q = g // 16, g // 4 % 4, g % 4
                w = 2 * (g // 4) + q // 2
                sl = w % 4
                if g < 2:
                    pe.wait_ge(s["z2_done"], 2 * b + 2)
                else:
                    pe.wait_ge(s["x1_done"], 32 * b + g - 1)
                pe.wait_ge(s[f"w_in{sl}"], 16 * (8 * b + 4 + w // 4 + 1))
                wr = w_ring[:, sl, :].rearrange("c (t k q o) -> c t k q o", t=2, k=2, q=2)
                for nh in range(2):
                    for ch in range(2):
                        for t, (wt, zt) in enumerate(((0, 0), (0, 1), (1, 0))):
                            ins = nc.tensor.matmul(PS[g % 2][:, 512 * nh:512 * nh + 512], wr[:, wt, ch, q % 2, :],
                                                   z2[:, zt, ch, 512 * nh:512 * nh + 512],
                                                   start=ch == 0 and t == 0, stop=ch == 1 and t == 2)
                ins.then_inc(s["un_mm"], 1)

            def unit(b, n):
                if n % 2:
                    pe.wait_ge(s["rows_done"], 16 * b + n)
                elif n > 0:
                    pe.wait_ge(s["o_done"], 8 * b + n // 2)
                for j in range(2):
                    pe.wait_ge(s[f"rows_in{j}"], 16 * (16 * b + n + 1))
                    for i in range(2):
                        t = 2 * j + i
                        ins = nc.tensor.matmul(unit_bank(n)[32 * t:32 * t + 32, :], cos_h[:, :],
                                               x_rows[:, j, 4 * i:4 * i + 4, :].rearrange("h c w -> h (c w)"),
                                               start=True, stop=True)
                    ins.then_inc(s["rows_mm"], 1)

            def turn_z2(b):
                pe.wait_ge(s["z2_done"], 2 * b + 2)
                pe.wait_ge(s["rows_done"], 16 * b + 16)
                for t in range(8):
                    at = PS[2][:, C * t:C * t + C] if t < 4 else PB[(t - 4) // 2][:, C * (t % 2):C * (t % 2) + C]
                    for ch in range(2):
                        for hl in range(2):
                            ins = nc.tensor.matmul(at[:, 128 * ch:128 * ch + 128], z2[:, hl, ch, 128 * t:128 * t + 128],
                                                   ident[:, :], start=hl == 0, stop=hl == 1)
                    if t in (3, 5, 7):
                        ins.then_inc(s["z2t_mm"], 1)

            def z2_sums(b):
                pe.wait_ge(s["z2t_done"], 3 * b + 3)
                pe.wait_ge(s["gate_in"], 48 * b + 48)
                for ch in range(2):
                    for t in range(8):
                        ins = nc.tensor.matmul(PB[1][:, 64 * ch:64 * ch + 64], z2t[:, t, 128 * ch:128 * ch + 128],
                                               basis[:, t, :], start=t == 0, stop=t == 7)
                ins.then_inc(s["zf_mm"], 1)

            def y_sums(b, g):
                oh, p, q = g // 16, g // 4 % 4, g % 4
                sl = g // 2 % 4
                if g == 0:
                    pe.wait_ge(s["zf_done"], b + 1)
                wr = w_ring[:, sl, :].rearrange("c (t k q o) -> c t k q o", t=2, k=2, q=2)
                for ch in range(2):
                    for wt in (0, 1) if ch == 0 else (1, 0):
                        zs = zf[:, ch, g % 16, 0:2 - wt, :].rearrange("p t f -> p (t f)")
                        ins = nc.tensor.matmul(PB[0][:, 8 * oh:8 * oh + 8 - 4 * wt], wr[:, wt, ch, q % 2, :], zs,
                                               start=g % 16 == 0 and ch == 0 and wt == 0,
                                               stop=g % 16 == 15 and ch == 1 and wt == 0)
                ins.then_inc(s["wu_used"], 1)

            def gate_mm(b, step):
                if step == 0:
                    tiny("mv1_done", 2 * b + 2, mv[:, :, 0], 4, "gm1_mm")
                elif step == 1:
                    tiny("dev1_done", 4 * b + 4, var, 6, "gv1_mm")
                elif step == 2:
                    pe.wait_ge(s["spec_done"], 2 * b + 1)
                    for ch in range(2):
                        ins = nc.tensor.matmul(small[0:HID, 16:20], mlp1[:, ch, :], spec[:, ch, :], start=ch == 0, stop=ch == 1)
                    ins.then_inc(s["y1_mm"], 1)
                else:
                    pe.wait_ge(s["hid1_done"], b + 1)
                    for oh in range(2):
                        ins = nc.tensor.matmul(small[:, 24 + 4 * oh:28 + 4 * oh], mlp2[:, 128 * oh:128 * oh + 128], hidden,
                                               start=True, stop=True)
                    ins.then_inc(s["y2_mm"], 1)

            def after(b, nxt):
                turn_z2(b)
                for g in range(32):
                    un_group(b, g)
                    if g == 1:
                        z2_sums(b)
                    if g >= 4:
                        y_sums(b, g - 4)
                for g in range(28, 32):
                    y_sums(b, g)
                for k in range(16):
                    if nxt:
                        embed_sub(b + 1, 2 * k)
                        embed_sub(b + 1, 2 * k + 1)
                    for step in {0: (0,), 1: (1,), 3: (2,), 4: (3,)}.get(k, ()):
                        gate_mm(b, step)

            pe.wait_ge(s["prep"], 1)
            tiny("stat_done", 2, mv[:, :, 0], 0, "gm_mm")
            tiny("dev_done", 4, var, 2, "gv_mm")
            for e in range(32):
                embed_sub(0, e)

            def batch(b, nxt):
                attention(b, nxt)
                after(b, nxt)

            batches(pe, batch)


def kernel(**inputs):
    import math
    import numpy as np
    import concourse.bacc as bacc
    from concourse.bass_utils import run_bass_kernel_spmd

    def dct_rows(n):
        i = np.arange(n, dtype=np.float32)[:, None]
        j = np.arange(n, dtype=np.float32)[None, :]
        m = np.cos(math.pi * j * (2.0 * i + 1.0) / (2.0 * n)) * math.sqrt(2.0 / n)
        m[0] *= math.sqrt(0.5)
        return m[0:2].astype(np.float32)

    g = {k: np.asarray(v) for k, v in inputs.items()}
    c = np.ascontiguousarray

    def columns(vec):
        return c(vec.reshape(-1, 128).T)

    ah, aw = dct_rows(H), dct_rows(W)
    cos_h = np.zeros((H, 32), np.float32)
    cos_h[:, 0:2] = ah.T
    r = (np.arange(REL, dtype=np.float32) - np.float32(HP - 1)) / np.float32(HP - 1)
    grid = np.einsum("uhp,vwq->hwpquv", ah.reshape(2, HP, PT), aw.reshape(2, WP_, PT)).reshape(8, 128, 4 * PT * PT)
    rel = np.stack([np.repeat(r, REL), np.tile(r, REL), np.ones(REL * REL, np.float32)])
    arrays = {
        "x": g["x"],
        "w_embed": c(g["L0_conv_w_embed"].transpose(1, 2, 3, 0)).reshape(C, PT, PT * C),
        "w_unembed": c(g["L0_conv_w_unembed"].transpose(0, 2, 3, 1)).reshape(C, PT, PT * C),
        "w_qkvt": c(g["L0_conv_w_qkv"].T), "w_projt": c(g["L0_conv_w_proj"].T),
        "b_embed": columns(g["L0_conv_b_embed"]), "b_unembed": columns(g["L0_conv_b_unembed"]),
        "b_proj": columns(g["L0_conv_b_proj"]), "b_v": columns(g["L0_conv_b_qkv"][2 * C:]),
        "b_qk": columns(g["L0_conv_b_qkv"][:2 * C]),
        "cpb_w1t": c(g["L0_conv_cpb_w1"].T), "cpb_b1": g["L0_conv_cpb_b1"].reshape(1, CPB),
        "cpb_w2t": c(g["L0_conv_cpb_w2"].T),
        "w1t": c(g["L1_conv_w1"].T), "w2t": c(g["L1_conv_w2"].T),
        "identity": np.eye(128, dtype=np.float32),
        "group_mean": np.kron(np.eye(16, dtype=np.float32), np.full((8, 8), 0.125, np.float32)),
        "basis": c(grid.transpose(1, 0, 2)), "cos_h": cos_h, "cos_w": c(np.broadcast_to(aw[None], (128, 2, W))), "rel": rel,
    }
    sums = [float(ah[u].astype(np.float64).sum() * aw[w].astype(np.float64).sum()) for u in range(2) for w in range(2)]
    nc = bacc.Bacc("TRN2", target_bir_lowering=False, num_devices=1)
    aps = {k: nc.dram_tensor("in_" + k, v.shape, mybir.dt.from_np(v.dtype), kind="ExternalInput").ap()
           for k, v in arrays.items()}
    aps["out"] = nc.dram_tensor("x_out", (B, C, H, W), mybir.dt.float32, kind="ExternalOutput").ap()
    build(nc, aps, sums)
    res = run_bass_kernel_spmd(nc, [{"in_" + k: v for k, v in arrays.items()}], core_ids=[0])
    return res.results[0]["x_out"]
```

```python
import concourse.bass as bass
from concourse import mybir
from contextlib import ExitStack

B, C, H, W = 8, 256, 128, 128
PT = 4
HP, WP_ = H // PT, W // PT
N = HP * WP_
NH_, HD = 8, 32
HID = C // 4
CPB = 512
REL = 2 * HP - 1
UB = (2 * HP - PT) * WP_
GN_EPS = 1e-5


def build(nc, a, plane_sums):
    f32, f32r, bf16 = mybir.dt.float32, mybir.dt.float32r, mybir.dt.bfloat16
    ALU, ACT = mybir.AluOpType, mybir.ActivationFunctionType
    AX = mybir.AxisListType
    SCALE = float(HD) ** -0.5

    d_tab = nc.dram_tensor("bias_table", [2, NH_, REL * REL], f32, kind="Internal").ap()
    d_bt = nc.dram_tensor("bias_split", [NH_, 128, 2, UB], f32, kind="Internal").ap()
    d_mt = nc.dram_tensor("bias_for_max", [NH_, 128, UB], bf16, kind="Internal").ap()

    x, out = a["x"], a["out"]
    xv = x.rearrange("b c (hp p) w -> b c hp p w", p=PT)

    ctx = ExitStack()
    with ctx:
        def region(*layouts):
            seen, most = {}, 0
            for layout in layouts:
                with ExitStack() as piece:
                    size = 0
                    for name, shape, dt in layout:
                        seen[name] = piece.enter_context(nc.sbuf_tensor(name, shape, dt))
                        k = 2 if dt == bf16 else 4
                        for s in shape[1:]:
                            k *= s
                        size += (k + 31) // 32 * 32
                    most = max(most, size)
            ctx.enter_context(nc.sbuf_tensor("hold_" + layouts[0][0][0], [128, most // 4], f32))
            return seen

        r = region(
            [("x1", [128, 2, H * W], f32)],
            [("bias_t", [128, 2, 2, 2, UB], f32r), ("max_t0", [128, UB], bf16),
             ("q_stack", [128, NH_, N], f32r), ("k_stack", [128, NH_, N], f32r)],
            [("eighths_0_1", [128, 8192], f32), ("qk", [128, 4, N], f32)],
            [("raw", [128, 2, UB], f32), ("raw_h", [128, 2, UB], f32r), ("raw_l", [128, 2, UB], f32r),
             ("rel", [3, REL * REL], f32), ("hid", [128, 2, 512], f32), ("tab", [NH_, REL * REL], f32),
             ("tab_rev", [NH_, REL * REL], f32), ("cpb1", [3, CPB], f32), ("cpb2", [128, 4, NH_], f32),
             ("raw_m", [128, 2, UB], bf16), ("ident0", [128, 128], f32)])
        x1, bias_t, q_stack, k_stack = r["x1"], r["bias_t"], r["q_stack"], r["k_stack"]
        qk = r["qk"]
        pro = r
        x1v = x1[:, :, :].rearrange("c o (hp p wp q) -> c o p q hp wp", p=PT, wp=WP_, q=PT)
        x1r = x1[:, :, :].rearrange("c o (hp p w) -> c o p hp w", p=PT, w=W)
        xs = region([("x_stream", [128, 2, 2048], f32)])["x_stream"]
        r = region([("x_rows", [128, 2, 8, W], f32)],
                   [("basis", [128, 8, 4 * PT * PT], f32), ("mlp1", [128, 2, HID], f32), ("mlp2", [HID, C], f32),
                    ("zf", [128, 2, PT * PT, 2, 4], f32r)])
        x_rows, basis, mlp1, mlp2, zf = r["x_rows"], r["basis"], r["mlp1"], r["mlp2"], r["zf"]
        r = region([("x_split", [128, 2, 2, 2, 512], f32r)],
                   [("prob", [128, 2, 1024], f32), ("v", [128, 8, NH_, 2 * HD], f32)],
                   [("pad", [128, 2048], f32), ("z2", [128, 2, 2, N], f32r)])
        x_split, prob, v, z2 = r["x_split"], r["prob"], r["v"], r["z2"]
        r = region([("w_ring", [128, 4, 1024], f32r)], [("w_raw", [128, 4, 1024], f32)],
                   [("w_qkv", [128, 2, 3 * C], f32), ("dump", [128, N], bf16), ("w_proj", [128, 2, C], f32),
                    ("max_t1", [128, UB], bf16), ("unit_rows", [128, 512], f32)])
        w_raw, w_ring, w_qkv, w_proj, dump, unit_rows = r["w_raw"], r["w_ring"], r["w_qkv"], r["w_proj"], r["dump"], r["unit_rows"]
        max_t = [pro["max_t0"], r["max_t1"]]
        r = region([("z", [128, 2, N], f32)], [("z2t", [128, 8, C], f32)], [("x_third", [128, 2048], f32)])
        z, z2t = r["z"], r["z2t"]
        xbuf = [xs[:, 0, :], xs[:, 1, :], r["x_third"][:, :]]

        def sb(name, shape, dt=f32):
            return ctx.enter_context(nc.sbuf_tensor(name, shape, dt))

        rows = sb("rows", [128, 512])
        row_sums = sb("row_sums", [128, 2, 2, W])
        ident = sb("ident", [128, 128], f32r)
        group = sb("group", [128, 128])
        cos_w = sb("cos_w", [128, 2, W])
        cos_h = sb("cos_h", [128, 32])
        bn = sb("bn", [128, 32, 6])
        neg_max = sb("neg_max", [16, 128], f32r)
        mx = sb("mx", [128, 2, 16])
        vec = sb("vec", [128, 64])
        b_embed, b_un, b_proj, b_v = (vec[:, 2 * i:2 * i + 2] for i in range(4))
        b_qk = vec[:, 8:12]
        b_qks = vec[:, 12:16]
        mv = vec[:, 16:20].rearrange("p (c t) -> p c t", t=2)
        dev, var, veps, power = (vec[:, 20 + 2 * i:22 + 2 * i] for i in range(4))
        rstd, shift = vec[:, 28:30], vec[:, 30:32]
        spec = vec[:, 32:40].rearrange("p (o f) -> p o f", f=4)
        gsum, gexp, gate, gr = (vec[:, 40 + 2 * i:42 + 2 * i] for i in range(4))
        scale1, shift1 = vec[:, 48:50], vec[:, 50:52]
        hidden = vec[0:HID, 52:56]
        rstd1, negm1 = vec[:, 56:58], vec[:, 58:60]
        mean, gneg = vec[:, 60:62], vec[:, 62:64]

        PS = [ctx.enter_context(nc.psum_tensor(f"wide{i}", [128, 1024], f32)) for i in range(3)]
        PB = [ctx.enter_context(nc.psum_tensor(f"bank{i}", [128, 512], f32)) for i in range(2)]
        small = PS[2]

        def sem(name):
            return ctx.enter_context(nc.semaphore(name))

        s = {}
        for name in (
            "const_in raw_in0 raw_in1 raw_out0 raw_out1 tab_out xs_in0 xs_in1 xs_in2 w_in0 w_in1 w_in2 w_in3 "
            "wqkv_in proj_in stack_in0 stack_in1 bias_in0 bias_in1 maxt_in0 maxt_in1 nmax_in "
            "xr_in0 xr_in1 xr_in2 xr_in3 xr_in4 xr_in5 xr_in6 xr_in7 rows_in0 rows_in1 sums_in gate_in out_first out_last "
            "ident_done raw_h_done raw_l_done wh_done we_done wu_done hid_mm hid_done tab_mm tab_done rev_done bp_mm prep "
            "split_used qk_mm v_mm smax_mm tr_mm score_mm prob_used proj_mm un_mm rows_mm z2t_mm zf_mm wu_used "
            "gm_mm gv_mm gm1_mm gv1_mm y1_mm y2_mm "
            "norm_done z_done qk_done high_done v_done exp_done z2h_done rows_done z2t_done zfh_done hid1_done gexp_done "
            "h_done split_done low_done max_done nmax_done recip_done o_done z2_done x1_done bn_done "
            "chunk_done stat_done dev_done veps_done coef_done mv1_done dev1_done veps1_done spec_link spec_done zf_done gate_link gate_done "
            "ones_done kone_done power_done rstd_done rstd1_done final_done passed"
        ).split():
            s[name] = sem(name)

        block = ctx.enter_context(nc.Block())

        def positive(count):
            return not isinstance(count, int) or count > 0

        def max_tiles(step):
            return min(16, step + 1 + (step >= 6) + (step >= 8))

        RAW = 2 * NH_
        RAW_LOW = NH_

        def first(b):
            return isinstance(b, int) and b == 0

        def batches(eng, step):
            step(0, True)
            with eng.Fori(1, B - 1) as b:
                step(b, True)
            step(B - 1, False)

        def raw_in_total(n):
            return 16 * 4 * (n // 2 + 1)

        def raw_out_total(sl, count):
            return 16 * sum(2 if m < RAW_LOW else 1 for m in range(sl, count, 2))

        XS_IN = (8 + 6, 8 + 5, 5)

        def chunk_loads(b, k):
            return 16 * (XS_IN[k % 3] * b + (8 if k % 3 < 2 else 0) + k // 3 + 1)

        OUT_ORDER = (4, 5, 6, 7, 3, 2, 1, 0)

        UNIT_STEPS = (5, 8, 12, 15)

        def unit_bank(n):
            return PB[1 - n % 4 // 2]

        HALF = (0, 2, 1, 3)

        def max_bank(j, t):
            return PS[2] if j else PS[(2, 1, 0)[t % 3]]

        def raw_part(n):
            return pro["raw"][:, n % 2, ::-1]

        @block.sync
        def _(sp):
            def const(dst, src):
                sp.dma_start(dst, src).then_inc(s["const_in"], 16)

            const(pro["ident0"][:, :], a["identity"])
            const(group[:, :], a["group_mean"])
            const(cos_w[:, :, :], a["cos_w"])
            const(cos_h[:, :], a["cos_h"])
            const(pro["rel"][:, :], a["rel"])
            const(pro["cpb1"][0:2, :], a["cpb_w1t"])
            const(pro["cpb1"][2:3, :], a["cpb_b1"])
            const(pro["cpb2"][:, :, :], a["cpb_w2t"].rearrange("(t p) h -> p t h", p=128))
            const(b_embed, a["b_embed"])
            const(b_un, a["b_unembed"])
            const(b_proj, a["b_proj"])
            const(b_v, a["b_v"])
            const(b_qk, a["b_qk"])
            sp.dma_start(w_proj[:, :, :], a["w_projt"].rearrange("(k p) o -> p k o", p=128)).then_inc(s["proj_in"], 16)

            def raw_load(n):
                sl = n % 2
                if n == 0:
                    sp.wait_ge(s["tab_out"], 32)
                if n >= 2:
                    sp.wait_ge(s["raw_h_done"], n - 1)
                    sp.wait_ge(s["raw_l_done"], min(n - 1, RAW_LOW))
                t, h = divmod(n, NH_)
                for i in range(4):
                    src = bass.AP(d_tab.tensor, ((1 - t) * NH_ + h) * REL * REL + i * REL,
                                  [[1, 32], [REL, UB // WP_], [1, WP_]])
                    sp.dma_start(pro["raw"][32 * i:32 * i + 32, sl, :].rearrange("p (r c) -> p r c", c=WP_), src)\
                        .then_inc(s[f"raw_in{sl}"], 16)

            def raw_store(n):
                sl = n % 2
                inc = s[f"raw_out{sl}"]
                sp.wait_ge(s["raw_h_done"], n + 1)
                if n >= RAW_LOW:
                    sp.dma_start(d_mt[n - RAW_LOW], pro["raw_m"][:, sl, :]).then_inc(inc, 16)
                    return
                sp.wait_ge(s["raw_l_done"], n + 1)
                for t, part in enumerate((pro["raw_h"], pro["raw_l"])):
                    sp.dma_start(d_bt[n, :, t, :], part[:, sl, :].bitcast(f32)).then_inc(inc, 16)

            def load_stats(b, k):
                if k >= 2:
                    sp.wait_ge(s["chunk_done"], 16 * b + k - 1)
                elif not first(b):
                    sp.wait_ge(s["split_done"], 32 * (b - 1) + 2 * (15, 13)[k] + 2)
                ch, kk = divmod(k, 8)
                src = x[b, ch * 128:ch * 128 + 128, kk * 16:kk * 16 + 16, :]
                sp.dma_start(xbuf[k % 2].rearrange("c (h w) -> c h w", w=W), src).then_inc(s[f"xs_in{k % 2}"], 16)

            def load_embed_x(b, k):
                if k >= 3:
                    sp.wait_ge(s["split_done"], 32 * b + 2 * (k - 3) + 2)
                elif k < 2:
                    sp.wait_ge(s["chunk_done"], 16 * b + 15 + k)
                elif not first(b):
                    sp.wait_ge(s["zf_mm"], b)
                (ch, p), nh = divmod(k // 2, 4), k % 2
                src = xv[b, ch * 128:ch * 128 + 128, nh * 16:nh * 16 + 16, p, :]
                sp.dma_start(xbuf[k % 3].rearrange("c (h w) -> c h w", w=W), src).then_inc(s[f"xs_in{k % 3}"], 16)

            def load_embed_w(b, w):
                i, qp = divmod(w, 2)
                if w >= 4:
                    sp.wait_ge(s["split_used"], 32 * b + 4 * (i - 2) + 3 + qp)
                elif not first(b):
                    sp.wait_ge(s["wu_used"], 32 * (b - 1) + 2 * (12 + w) + 2)
                else:
                    sp.wait_ge(s["bp_mm"], 1)
                sp.dma_start(w_raw[:, w % 4, 512:1024], a["w_embed"][w])\
                    .then_inc(s[f"w_in{w % 4}"], 16)

            def load_un_w(b, w):
                if w >= 4:
                    sp.wait_ge(s["wu_used"], 32 * b + 2 * (w - 4) + 2)
                elif w == 0:
                    sp.wait_ge(s["v_mm"], 2 * b + 2)
                elif w == 1:
                    sp.wait_ge(s["max_done"], 64 * b + 64)
                elif w == 2:
                    sp.wait_ge(s["proj_mm"], 2 * b + 2)
                else:
                    sp.wait_ge(s["sums_in"], 16 * (32 * b + 32))
                sp.dma_start(w_raw[:, w % 4, 512:1024], a["w_unembed"][w])\
                    .then_inc(s[f"w_in{w % 4}"], 16)

            def load_unit(b, n):
                if n == 0:
                    if positive(b):
                        sp.wait_ge(s["y2_mm"], b)
                for j in range(2):
                    if n > 0:
                        sp.wait_ge(s["rows_mm"], 32 * b + 2 * n + j - 1)
                    c0 = 16 * n + 8 * j
                    sp.dma_start(x_rows[:, j, :, :], x[b, c0:c0 + 8, :, :].rearrange("c h w -> h c w"))\
                        .then_inc(s[f"rows_in{j}"], 16)

            def embed(b, k):
                load_embed_x(b, k)
                if k == 2:
                    for w in range(4):
                        load_embed_w(b, w)
                if k % 2 and k >= 5:
                    load_embed_w(b, k - 1)
                    load_embed_w(b, k)

            def load_qkv_w(b):
                sp.wait_ge(s["split_used"], 32 * b + 28)
                sp.dma_start(w_qkv[:, :, :], a["w_qkvt"].rearrange("(k p) o -> p k o", p=128)).then_inc(s["wqkv_in"], 16)

            def load_max_t(b, h):
                if h >= 2:
                    sp.wait_ge(s["max_done"], 64 * b + 8 * (h - 1))
                sp.dma_start(max_t[h % 2][:, :], d_mt[h]).then_inc(s[f"maxt_in{h % 2}"], 16)

            def load_bias(b, j):
                if j >= 2:
                    sp.wait_ge(s["score_mm"], 64 * b + 16 * (j - 1))
                for hd in range(2):
                    sp.dma_start(bias_t[:, j % 2, hd, :, :].bitcast(f32), d_bt[2 * j + hd]).then_inc(s[f"bias_in{j % 2}"], 16)

            def attention(b, nxt):
                sp.wait_ge(s["split_used"], 32 * b + 32)
                sp.dma_start(w_proj[:, :, :], a["w_projt"].rearrange("(k p) o -> p k o", p=128)).then_inc(s["proj_in"], 16)
                if positive(b):
                    sp.wait_ge(s["out_first"], 96 * b)
                load_max_t(b, 0)
                load_max_t(b, 1)
                for n in range(4):
                    sp.wait_ge(s["high_done"], 16 * b + 4 * n + 4)
                    i = HALF[n]
                    stack, to = (q_stack, 32) if i < 2 else (k_stack, 64)
                    heads = slice(4 * (i % 2), 4 * (i % 2) + 4)
                    sp.dma_start(stack[to:to + 32, heads, :].bitcast(f32), stack[0:32, heads, :].bitcast(f32))\
                        .then_inc(s[f"stack_in{n // 2}"], 16)
                    if n == 1:
                        if positive(b):
                            sp.wait_ge(s["out_last"], 32 * b)
                        load_bias(b, 0)
                        load_unit(b, 0)
                def stats(k):
                    if nxt and k < 16:
                        load_stats(b + 1, k)

                stats(0)
                stats(1)
                load_max_t(b, 2)
                load_max_t(b, 3)

                for j in range(4):
                    if j in (1, 2):
                        load_bias(b, j + 1)
                    stats(4 * j + 2)
                    load_unit(b, 4 * j + 1)
                    if j == 0:
                        sp.wait_ge(s["low_done"], 16 * b + 16)
                        load_bias(b, 1)
                    stats(4 * j + 3)
                    load_unit(b, 4 * j + 2)
                    stats(4 * j + 4)
                    if j == 3:
                        load_un_w(b, 0)
                    load_unit(b, 4 * j + 3)
                    if j < 2:
                        load_max_t(b, 2 * j + 4)
                        load_max_t(b, 2 * j + 5)
                    stats(4 * j + 5)
                    if j < 3:
                        load_unit(b, 4 * j + 4)

            def unembed(b):
                sp.wait_ge(s["rows_mm"], 32 * b + 32)
                sp.dma_start(basis[:, :, :], a["basis"]).then_inc(s["gate_in"], 16)
                sp.dma_start(mlp1[:, :, :], a["w1t"].rearrange("(k p) o -> p k o", p=128)).then_inc(s["gate_in"], 16)
                sp.dma_start(mlp2[:, :], a["w2t"]).then_inc(s["gate_in"], 16)
                def load_x(i):
                    oh, p = divmod(i, 4)
                    sp.dma_start(x1r[:, oh, p], xv[b, oh * 128:oh * 128 + 128, :, p, :]).then_inc(s[f"xr_in{i}"], 16)

                load_un_w(b, 1)
                sp.wait_ge(s["prob_used"], 64 * b + 64)
                sp.wait_ge(s["max_done"], 64 * b + 64)
                load_x(0)
                load_un_w(b, 3)
                load_un_w(b, 2)
                load_x(1)
                load_x(2)
                for i in range(2, 8):
                    load_un_w(b, 2 * i)
                    if i + 1 < 8:
                        load_x(i + 1)
                    load_un_w(b, 2 * i + 1)

            def store(b, j):
                sp.wait_ge(s["final_done"], 8 * b + j + 1)
                oh, qt = divmod(OUT_ORDER[j], 4)
                sp.dma_start(out[b, oh * 128:oh * 128 + 128, 32 * qt:32 * qt + 32, :],
                             x1[:, oh, 4096 * qt:4096 * qt + 4096].rearrange("c (h w) -> c h w", w=W))\
                    .then_inc(s["out_first" if j < 6 else "out_last"], 16)

            for k in range(16):
                load_stats(0, k)
            sp.wait_ge(s["tab_done"], 8)
            sp.dma_start(d_tab[0], pro["tab"][:, :]).then_inc(s["tab_out"], 16)
            sp.wait_ge(s["rev_done"], 1)
            sp.dma_start(d_tab[1], pro["tab_rev"][:, :]).then_inc(s["tab_out"], 16)
            for k in range(16):
                embed(0, k)
                raw_load(k)
                if k >= 2:
                    raw_store(k - 2)
            load_qkv_w(0)
            raw_store(RAW - 2)
            raw_store(RAW - 1)
            for sl in range(2):
                sp.wait_ge(s[f"raw_out{sl}"], raw_out_total(sl, RAW))

            def batch(b, nxt):
                attention(b, nxt)
                unembed(b)
                for k in range(16):
                    if nxt:
                        embed(b + 1, k)
                    if k >= 13:
                        store(b, k - 13)
                if nxt:
                    load_qkv_w(b + 1)
                for j in range(3, 8):
                    store(b, j)

            batches(sp, batch)
            sp.wait_ge(s["out_first"], 96 * B)
            sp.wait_ge(s["out_last"], 32 * B)

        @block.gpsimd
        def _(pool):
            nc.gpsimd.memset(power, -0.5).then_inc(s["power_done"], 1)
            pool.wait_ge(s["power_done"], 1)

            def attention(b, nxt):
                pool.wait_ge(s["split_used"], 32 * b + 32)
                pool.nop().then_inc(s["passed"], 1)
                nc.gpsimd.memset(v[:, :, :, HD:2 * HD], 1.0).then_inc(s["ones_done"], 1)
                pool.wait_ge(s["ones_done"], b + 1)
                if first(b):
                    for sl in range(2):
                        pool.wait_ge(s[f"raw_out{sl}"], raw_out_total(sl, RAW))
                else:
                    pool.wait_ge(s["out_first"], 96 * b)
                    pool.nop().then_inc(s["passed"], 1)
                nc.gpsimd.memset(k_stack[96:97, :, :].bitcast(f32), 1.0).then_inc(s["kone_done"], 1)
                if nxt:
                    rstd_x(b + 1)

            def rstd_x(b):
                pool.wait_ge(s["veps_done"], b + 1)
                nc.gpsimd.tensor_tensor(rstd, veps, power, ALU.pow).then_inc(s["rstd_done"], 1)

            def tail(b):
                pool.wait_ge(s["veps1_done"], b + 1)
                nc.gpsimd.tensor_tensor(rstd1, veps, power, ALU.pow).then_inc(s["rstd1_done"], 1)
                pool.wait_ge(s["gate_done"], b + 1)
                pool.nop().then_inc(s["passed"], 1)
                for j in range(8):
                    oh, qt = divmod(OUT_ORDER[j], 4)
                    part = x1[:, oh, 4096 * qt:4096 * qt + 4096]
                    nc.gpsimd.tensor_scalar(part, part, scale1[:, oh:oh + 1], shift1[:, oh:oh + 1],
                                            ALU.mult, ALU.add).then_inc(s["final_done"], 1)

            rstd_x(0)

            def unembed_weights_low(b):
                for w in range(16):
                    pool.wait_ge(s["wh_done"], 32 * b + 16 + w + 1)
                    nc.gpsimd.tensor_tensor(w_ring[:, w % 4, 512:1024], w_raw[:, w % 4, 512:1024],
                                            w_ring[:, w % 4, 0:512].bitcast(f32), ALU.subtract).then_inc(s["wu_done"], 1)

            def batch(b, nxt):
                attention(b, nxt)
                unembed_weights_low(b)
                tail(b)

            batches(pool, batch)

        @block.scalar
        def _(act):
            act.wait_ge(s["const_in"], 16 * 13)
            nc.scalar.activation(ident[:, :], pro["ident0"][:, :], ACT.Identity).then_inc(s["ident_done"], 1)
            nc.scalar.activation(b_qks[:, 0:2], b_qk[:, 0:2], ACT.Identity, scale=SCALE).then_inc(s["ident_done"], 1)
            nc.scalar.activation(b_qks[:, 2:4], b_qk[:, 2:4], ACT.Identity).then_inc(s["ident_done"], 1)
            for m in range(32):
                act.wait_ge(s["hid_mm"], m + 1)
                if m >= 2:
                    act.wait_ge(s["tab_mm"], m - 1)
                nb = min(512, REL * REL - 512 * (m // 4))
                nc.scalar.activation(pro["hid"][:, m % 2, 0:nb], PB[m % 2][:, 0:nb], ACT.Relu)\
                    .then_inc(s["hid_done"], 1)

            def raw_high(n):
                sl = n % 2
                act.wait_ge(s[f"raw_in{sl}"], raw_in_total(n))
                if n >= 2:
                    act.wait_ge(s[f"raw_out{sl}"], raw_out_total(sl, n - 1))
                dst = pro["raw_h"] if n < RAW_LOW else pro["raw_m"]
                nc.scalar.activation(dst[:, sl, :], raw_part(n), ACT.Identity).then_inc(s["raw_h_done"], 1)

            def weights_high(b, u, w):
                act.wait_ge(s[f"w_in{w % 4}"], 16 * (8 * b + 4 * u + w // 4 + 1))
                nc.scalar.activation(w_ring[:, w % 4, 0:512], w_raw[:, w % 4, 512:1024], ACT.Identity)\
                    .then_inc(s["wh_done"], 1)

            def embed_weights_high(b, k):
                if k % 2 == 0:
                    weights_high(b, 0, k)
                    weights_high(b, 0, k + 1)

            def normalise(b, k):
                sl, ch = k % 3, k // 8
                if k == 0:
                    act.wait_ge(s["coef_done"], b + 1)
                act.wait_ge(s[f"xs_in{sl}"], chunk_loads(b, k))
                nc.scalar.activation(xbuf[sl], xbuf[sl], ACT.Identity, bias=shift[:, ch:ch + 1],
                                     scale=rstd[:, ch:ch + 1]).then_inc(s["norm_done"], 1)

            def move_max(b, j):
                act.wait_ge(s["nmax_done"], 4 * b + j + 1)
                act.dma_start(q_stack[96:97, 2 * j:2 * j + 2, :].bitcast(f32),
                              neg_max[:, :].bitcast(f32)).then_inc(s["nmax_in"], 16)

            def attention(b):
                for oh in range(2):
                    act.wait_ge(s["split_used"], 32 * b + 32)
                    nc.scalar.activation(z[:, oh, :], PS[oh][:, :], ACT.Identity, bias=b_embed[:, oh:oh + 1])\
                        .then_inc(s["z_done"], 1)
                if first(b):
                    for sl in range(2):
                        act.wait_ge(s[f"raw_out{sl}"], raw_out_total(sl, RAW))
                else:
                    act.wait_ge(s["out_first"], 96 * b)
                for n in range(4):
                    i = HALF[n]
                    act.wait_ge(s["qk_mm"], 4 * b + n + 1)
                    nc.scalar.activation(qk[:, i, :], PS[n % 2][:, :], ACT.Identity, bias=b_qks[:, i:i + 1],
                                         scale=SCALE if i < 2 else 1.0).then_inc(s["qk_done"], 1)
                    act.wait_ge(s["qk_done"], 4 * b + n + 1)
                    stack = q_stack if i < 2 else k_stack
                    for k in range(4):
                        nc.scalar.activation(stack[0:32, 4 * (i % 2) + k, :], qk[32 * k:32 * k + 32, i, :], ACT.Identity)\
                            .then_inc(s["high_done"], 1)
                for i in range(2):
                    act.wait_ge(s["v_mm"], 2 * b + i + 1)
                    nc.scalar.activation(v[:, 4 * i:4 * i + 4, :, 0:HD],
                                         PS[i][:, :].rearrange("p (t h d) -> p t h d", t=4, d=HD), ACT.Identity)\
                        .then_inc(s["v_done"], 1)
                move_max(b, 0)
                for n in range(64):
                    act.wait_ge(s["score_mm"], 64 * b + n + 1)
                    if n >= 2:
                        act.wait_ge(s["prob_used"], 64 * b + n - 1)
                    nc.scalar.activation(prob[:, n % 2, :], PS[n % 2][:, :], ACT.Exp).then_inc(s["exp_done"], 1)
                    if n % 16 == 14 and n < 48:
                        move_max(b, n // 16 + 1)
                    if n % 16 in UNIT_STEPS:
                        unit_out(b, 4 * (n // 16) + UNIT_STEPS.index(n % 16))
                weights_high(b, 1, 0)
                weights_high(b, 1, 1)
                for oh in range(2):
                    act.wait_ge(s["proj_mm"], 2 * b + oh + 1)
                    nc.scalar.activation(z2[:, 0, oh, :], PS[oh][:, :], ACT.Identity, bias=b_proj[:, oh:oh + 1])\
                        .then_inc(s["z2h_done"], 1)

            def unit_out(b, n):
                act.wait_ge(s["rows_mm"], 2 * (16 * b + n) + 2)
                if n > 0:
                    act.wait_ge(s["sums_in"], 16 * (32 * b + 2 * n))
                elif positive(b):
                    act.wait_ge(s["spec_done"], 2 * b)
                nc.scalar.activation(unit_rows[:, :], unit_bank(n)[:, :], ACT.Identity).then_inc(s["rows_done"], 1)
                act.wait_ge(s["rows_done"], 16 * b + n + 1)
                oh, cu = divmod(16 * n, 128)
                for u in range(2):
                    act.dma_start(row_sums[cu:cu + 16, oh, u, :], unit_rows[u:u + 97:32, :]).then_inc(s["sums_in"], 16)

            def z2_turned(b):
                for i, src in enumerate((PS[2][:, :], PB[0][:, :], PB[1][:, :])):
                    act.wait_ge(s["z2t_mm"], 3 * b + i + 1)
                    t0 = (0, 4, 6)[i]
                    t1 = (4, 6, 8)[i]
                    nc.scalar.activation(z2t[:, t0:t1, :].rearrange("p t k -> p (t k)"), src, ACT.Identity)\
                        .then_inc(s["z2t_done"], 1)
                act.wait_ge(s["zf_mm"], b + 1)
                nc.scalar.activation(zf[:, :, :, 0, :], PB[1][:, 0:128].rearrange("p (k g f) -> p k g f", k=2, f=4), ACT.Identity)\
                    .then_inc(s["zfh_done"], 1)

            def gate_steps(b, step):
                if step == 0:
                    act.wait_ge(s["y1_mm"], b + 1)
                    nc.scalar.activation(hidden, small[0:HID, 16:20], ACT.Relu).then_inc(s["hid1_done"], 1)
                else:
                    act.wait_ge(s["spec_done"], 2 * b + 2)
                    nc.scalar.activation(gexp, gneg, ACT.Exp).then_inc(s["gexp_done"], 1)

            def after(b, nxt):
                z2_turned(b)
                for w in range(2, 16):
                    weights_high(b, 1, w)
                for k in range(16):
                    if nxt:
                        normalise(b + 1, k)
                        embed_weights_high(b + 1, k)
                    if k == 3:
                        gate_steps(b, 0)
                    if k == 5:
                        gate_steps(b, 1)

            act.wait_ge(s["ident_done"], 3)
            act.wait_ge(s["prep"], 1)
            for k in range(16):
                normalise(0, k)
                embed_weights_high(0, k)
                if k >= 1:
                    raw_high(k - 1)
            raw_high(RAW - 1)

            def batch(b, nxt):
                attention(b)
                after(b, nxt)

            batches(act, batch)

        @block.vector
        def _(dve):
            def link(ins, name, value):
                ins.then_inc(s[name], 1)
                dve.wait_ge(s[name], value)

            dve.wait_ge(s["const_in"], 16 * 13)
            def raw_low(n):
                sl = n % 2
                dve.wait_ge(s["raw_h_done"], n + 1)
                if n >= 2:
                    dve.wait_ge(s[f"raw_out{sl}"], raw_out_total(sl, n - 1))
                nc.vector.tensor_tensor(pro["raw_l"][:, sl, :], raw_part(n), pro["raw_h"][:, sl, :].bitcast(f32),
                                        ALU.subtract).then_inc(s["raw_l_done"], 1)

            def weights_low(b, w):
                dve.wait_ge(s["wh_done"], 32 * b + w + 1)
                nc.vector.tensor_tensor(w_ring[:, w % 4, 512:1024], w_raw[:, w % 4, 512:1024],
                                        w_ring[:, w % 4, 0:512].bitcast(f32), ALU.subtract).then_inc(s["we_done"], 1)

            def embed_weights_low(b, k):
                if k == 0:
                    weights_low(b, 0)
                    weights_low(b, 1)
                elif k % 2 and k < 15:
                    weights_low(b, k + 1)
                    weights_low(b, k + 2)

            def stats_sum(b, k):
                for i in range(4):
                    stats_part(b, k, i)

            def stats_part(b, k, i):
                sl, ch = k % 2, k // 8
                if i == 0:
                    dve.wait_ge(s[f"xs_in{sl}"], 16 * (XS_IN[sl] * b + k // 2 + 1))
                ins = nc.vector.bn_stats(bn[:, 4 * (k % 8) + i, :], xs[:, sl, 512 * i:512 * i + 512])
                if i == 3:
                    ins.then_inc(s["chunk_done"], 1)
                if i == 3 and k % 8 == 7:
                    dve.wait_ge(s["chunk_done"], 16 * b + k + 1)
                    dve.nop().then_inc(s["passed"], 1)
                    link(nc.vector.bn_aggr(mv[:, ch, :], bn[:, :, :].rearrange("p n t -> p (n t)")),
                         "stat_done", 2 * b + ch + 1)

            def group_dev(b, name, col):
                link(nc.vector.tensor_copy(mean, small[:, col:col + 2]), name, 4 * b + 1)
                link(nc.vector.tensor_tensor(dev, mv[:, :, 0], mean, ALU.subtract), name, 4 * b + 2)
                link(nc.vector.tensor_tensor(var, dev, dev, ALU.mult), name, 4 * b + 3)
                link(nc.vector.tensor_tensor(var, var, mv[:, :, 1], ALU.add), name, 4 * b + 4)

            def group_var(b, mm, done, col):
                dve.wait_ge(s[mm], b + 1)
                nc.vector.tensor_scalar(veps, small[:, col:col + 2], GN_EPS, None, ALU.add).then_inc(s[done], 1)

            def deviations(b):
                dve.wait_ge(s["gm_mm"], b + 1)
                group_dev(b, "dev_done", 0)

            def coefficients(b):
                group_var(b, "gv_mm", "veps_done", 2)
                dve.wait_ge(s["rstd_done"], b + 1)
                nc.vector.scalar_tensor_tensor(shift, mean, -1.0, rstd, ALU.mult, ALU.mult).then_inc(s["coef_done"], 1)

            def split(b, e):
                k, qp = divmod(e, 2)
                hs = e % 2
                src = xbuf[k % 3].rearrange("c (t q) -> c q t", q=PT)[:, 2 * qp:2 * qp + 2, :]
                if qp == 0:
                    dve.wait_ge(s["norm_done"], 16 * b + k + 1)
                if e >= 2:
                    dve.wait_ge(s["split_used"], 32 * b + e - 1)
                elif e == 1 and not first(b):
                    dve.wait_ge(s["un_mm"], 32 * b)
                nc.vector.tensor_copy(x_split[:, hs, 0, :, :], src).then_inc(s["h_done"], 1)
                dve.wait_ge(s["h_done"], 32 * b + e + 1)
                nc.vector.tensor_tensor(x_split[:, hs, 1, :, :], src, x_split[:, hs, 0, :, :].bitcast(f32),
                                        ALU.subtract).then_inc(s["split_done"], 1)

            def attention(b, nxt):

                def maximum(j, t):
                    hd, nt = divmod(t, 8)
                    h = 2 * j + hd
                    dve.wait_ge(s[f"maxt_in{h % 2}"], 16 * (4 * b + h // 2 + 1))
                    dve.wait_ge(s["smax_mm"], 64 * b + 16 * j + t + 1)
                    off = (HP - 4 - 4 * nt) * WP_
                    if positive(64 * b + 16 * j + t):
                        dve.wait_ge(s["max_done"], 64 * b + 16 * j + t)
                        dve.nop().then_inc(s["passed"], 1)
                    nc.vector.tensor_tensor_reduce(
                        out=dump[:, :], in0=max_bank(j, t)[:, :], in1=max_t[h % 2][:, off:off + N], scale=1.0, scalar=-3.0e38,
                        op0=ALU.add, op1=ALU.max, accum_out=mx[:, j % 2, t:t + 1]).then_inc(s["max_done"], 1)

                def negate(j):
                    dve.wait_ge(s["tr_mm"], 4 * b + j + 1)
                    if positive(16 * (4 * b + j)):
                        dve.wait_ge(s["nmax_in"], 16 * (4 * b + j))
                    nc.vector.tensor_scalar(neg_max[:, :], PS[2][0:16, 0:128], -1.0, None, ALU.mult)\
                        .then_inc(s["nmax_done"], 1)

                def normalise(j, nh, part):
                    n = 8 * b + 2 * j + nh
                    if part < 2:
                        if part == 0:
                            dve.wait_ge(s["prob_used"], 64 * b + 16 * j + 8 * nh + 8)
                            if positive(n):
                                dve.wait_ge(s["o_done"], n)
                        cols = slice(256 * part, 256 * part + 256)
                        nc.vector.reciprocal(rows[:, cols], PB[nh][:, cols]).then_inc(s["recip_done"], 1)
                        return
                    dve.wait_ge(s["recip_done"], 2 * n + 2)
                    for hd in range(2):
                        h = 2 * j + hd
                        ins = nc.vector.tensor_tensor(
                            z[32 * (h % 4):32 * (h % 4) + 32, h // 4, 512 * nh:512 * nh + 512],
                            PB[nh][64 * hd:64 * hd + 32, :], rows[64 * hd + 32:64 * hd + 64, :], ALU.mult)
                    ins.then_inc(s["o_done"], 1)

                def low_part(n, k):
                    i = HALF[n]
                    stack, to = (q_stack, 64) if i < 2 else (k_stack, 32)
                    h = 4 * (i % 2) + k
                    dve.wait_ge(s["high_done"], 16 * b + 4 * n + k + 1)
                    nc.vector.tensor_tensor(stack[to:to + 32, h, :], qk[32 * k:32 * k + 32, i, :],
                                            stack[0:32, h, :].bitcast(f32), ALU.subtract).then_inc(s["low_done"], 1)

                for n in range(8):
                    low_part(n // 4, n % 4)
                for t in range(16):
                    maximum(0, t)
                negate(0)
                for j in range(4):
                    done = 0
                    for step in range(16):
                        if j < 3:
                            want = max_tiles(step)
                            while done < want:
                                maximum(j + 1, done)
                                done += 1
                        if j == 0 and step < 8:
                            low_part(2 + step // 4, step % 4)
                        if step in (1, 2, 3) and j > 0:
                            normalise(j - 1, 1, step - 1)
                        if step in (9, 10, 11):
                            normalise(j, 0, step - 9)
                        if j < 3 and step == 14:
                            negate(j + 1)
                        if nxt:
                            stats_part(b + 1, 4 * j + step // 4, step % 4)
                if nxt:
                    deviations(b + 1)
                for part in range(3):
                    normalise(3, 1, part)
                if nxt:
                    coefficients(b + 1)
                for oh in range(2):
                    dve.wait_ge(s["z2h_done"], 2 * b + oh + 1)
                    nc.vector.scalar_tensor_tensor(z2[:, 1, oh, :], PS[oh][:, :], b_proj[:, oh:oh + 1],
                                                   z2[:, 0, oh, :].bitcast(f32), ALU.add, ALU.subtract)\
                        .then_inc(s["z2_done"], 1)
                gate_part(b, 5)

            def unembed(b, nxt):
                def x1_stats(g):
                    oh, p, q = g // 16, g // 4 % 4, g % 4
                    if q == 0:
                        dve.wait_ge(s["x1_done"], 32 * b + g + 4)
                    for i in range(2 * q, 2 * q + 2):
                        ins = nc.vector.bn_stats(bn[:, 8 * p + i, :], x1r[:, oh, p, 4 * i:4 * i + 4, :])
                    ins.then_inc(s["bn_done"], 1)
                    if g % 16 == 15:
                        dve.wait_ge(s["bn_done"], 32 * b + g + 1)
                        dve.nop().then_inc(s["passed"], 1)
                        link(nc.vector.bn_aggr(mv[:, oh, :], bn[:, :, :].rearrange("p n t -> p (n t)")),
                             "mv1_done", 2 * b + oh + 1)

                for g in range(32):
                    oh, p, q = g // 16, g // 4 % 4, g % 4
                    if q == 0:
                        dve.wait_ge(s[f"xr_in{g // 4}"], 16 * (b + 1))
                    dve.wait_ge(s["un_mm"], 32 * b + g + 1)
                    at = x1v[:, oh, p, q]
                    nc.vector.scalar_tensor_tensor(at, PS[g % 2][:, :].rearrange("c (h w) -> c h w", w=WP_),
                                                   b_un[:, oh:oh + 1], at, ALU.add, ALU.add).then_inc(s["x1_done"], 1)
                    if g == 1:
                        dve.wait_ge(s["zfh_done"], b + 1)
                        nc.vector.tensor_tensor(zf[:, :, :, 1, :], PB[1][:, 0:128].rearrange("p (k g f) -> p k g f", k=2, f=4),
                                                zf[:, :, :, 0, :].bitcast(f32), ALU.subtract).then_inc(s["zf_done"], 1)
                    if g >= 4:
                        x1_stats(g - 4)
                    if nxt and g == 29:
                        split(b + 1, 0)
                if nxt:
                    embed_weights_low(b + 1, 0)
                    split(b + 1, 1)
                for g in range(28, 32):
                    x1_stats(g)

            def gate_part(b, step):
                if step == 0:
                    dve.wait_ge(s["gm1_mm"], b + 1)
                    group_dev(b, "dev1_done", 4)
                elif step == 1:
                    group_var(b, "gv1_mm", "veps1_done", 6)
                elif step == 5:
                    dve.wait_ge(s["o_done"], 8 * b + 8)
                    dve.wait_ge(s["sums_in"], 16 * 32 * (b + 1))
                    for n in range(8):
                        oh, f = divmod(n, 4)
                        u, vv = divmod(f, 2)
                        link(nc.vector.tensor_tensor_reduce(
                            out=rows[:, 0:W], in0=row_sums[:, oh, u, :], in1=cos_w[:, vv, :], scale=1.0, scalar=0.0,
                            op0=ALU.mult, op1=ALU.add, accum_out=spec[:, oh, f:f + 1]), "spec_link", 15 * b + n + 1)
                elif step == 2:
                    dve.wait_ge(s["wu_used"], 32 * b + 32)
                    y_of = PB[0][:, 0:16].rearrange("p (o t f) -> p o t f", t=2, f=4)
                    for t in range(2):
                        link(nc.vector.tensor_tensor(spec, y_of[:, :, t, :], spec, ALU.add), "spec_link", 15 * b + 9 + t)
                    link(nc.vector.tensor_tensor(gneg, b_un, mean, ALU.subtract), "spec_link", 15 * b + 11)
                    for f in range(4):
                        link(nc.vector.scalar_tensor_tensor(spec[:, :, f], gneg, plane_sums[f], spec[:, :, f],
                                                            ALU.mult, ALU.add), "spec_link", 15 * b + 12 + f)
                    dve.wait_ge(s["rstd1_done"], b + 1)
                    for oh in range(2):
                        ins = nc.vector.tensor_scalar(spec[:, oh, :], spec[:, oh, :], rstd1[:, oh:oh + 1], None, ALU.mult)
                    ins.then_inc(s["spec_done"], 1)
                elif step == 3:
                    dve.wait_ge(s["y2_mm"], b + 1)
                    link(nc.vector.tensor_reduce(gsum, small[:, 24:32].rearrange("p (o f) -> p o f", f=4), AX.X, ALU.add),
                         "gate_link", 5 * b + 1)
                    nc.vector.tensor_scalar(gneg, gsum, -0.25, 80.0, ALU.mult, ALU.min).then_inc(s["spec_done"], 1)
                else:
                    dve.wait_ge(s["gexp_done"], b + 1)
                    link(nc.vector.tensor_scalar(gexp, gexp, 1.0, None, ALU.add), "gate_link", 5 * b + 2)
                    link(nc.vector.reciprocal(gate, gexp), "gate_link", 5 * b + 3)
                    link(nc.vector.tensor_tensor(gr, gate, rstd1, ALU.mult), "gate_link", 5 * b + 4)
                    link(nc.vector.tensor_scalar(scale1, gr, 1.0, None, ALU.add), "gate_link", 5 * b + 5)
                    nc.vector.scalar_tensor_tensor(shift1, mean, -1.0, gr, ALU.mult, ALU.mult).then_inc(s["gate_done"], 1)

            def after(b, nxt):
                for k in range(16):
                    for e in (2 * k, 2 * k + 1):
                        if nxt and e > 1:
                            split(b + 1, e)
                        if e in (2, 3, 5, 7, 9):
                            gate_part(b, (2, 3, 5, 7, 9).index(e))
                    if nxt and k > 0:
                        embed_weights_low(b + 1, k)

            for m in range(8):
                stats_sum(0, 2 * m)
                stats_sum(0, 2 * m + 1)
                dve.wait_ge(s["tab_mm"], 4 * m + 4)
                nb = min(512, REL * REL - 512 * m)
                nc.vector.tensor_copy(pro["tab"][:, 512 * m:512 * m + nb], PS[m % 2][0:NH_, 0:nb]).then_inc(s["tab_done"], 1)
            dve.wait_ge(s["tab_done"], 8)
            nc.vector.tensor_copy(pro["tab_rev"][:, :], pro["tab"][:, ::-1]).then_inc(s["rev_done"], 1)
            dve.wait_ge(s["bp_mm"], 1)
            nc.vector.tensor_tensor(b_proj, small[:, 0:2], b_proj, ALU.add).then_inc(s["prep"], 1)
            deviations(0)
            coefficients(0)
            for k in range(16):
                split(0, 2 * k)
                split(0, 2 * k + 1)
                if 1 <= k <= RAW_LOW:
                    raw_low(k - 1)
                embed_weights_low(0, k)

            def batch(b, nxt):
                attention(b, nxt)
                unembed(b, nxt)
                after(b, nxt)

            batches(dve, batch)

        @block.tensor
        def _(pe):
            pe.wait_ge(s["const_in"], 16 * 13)
            pe.wait_ge(s["proj_in"], 16)
            pe.wait_ge(s["ident_done"], 1)
            def columns(m):
                cb, kt = divmod(m, 4)
                return cb, kt, min(512, REL * REL - 512 * cb)

            def hidden_units(m):
                cb, kt, nb = columns(m)
                if m >= 2:
                    pe.wait_ge(s["hid_done"], m - 1)
                nc.tensor.matmul(PB[m % 2][:, 0:nb], pro["cpb1"][:, 128 * kt:128 * kt + 128],
                                 pro["rel"][:, 512 * cb:512 * cb + nb], start=True, stop=True).then_inc(s["hid_mm"], 1)

            hidden_units(0)
            for m in range(32):
                if m < 31:
                    hidden_units(m + 1)
                cb, kt, nb = columns(m)
                pe.wait_ge(s["hid_done"], m + 1)
                if kt == 0 and cb >= 2:
                    pe.wait_ge(s["tab_done"], cb - 1)
                nc.tensor.matmul(PS[cb % 2][0:NH_, 0:nb], pro["cpb2"][:, kt, :], pro["hid"][:, m % 2, 0:nb],
                                 start=kt == 0, stop=kt == 3).then_inc(s["tab_mm"], 1)
            for oh in range(2):
                for ch in range(2):
                    ins = nc.tensor.matmul(small[:, oh:oh + 1], w_proj[:, ch, 128 * oh:128 * oh + 128], b_v[:, ch:ch + 1],
                                           start=ch == 0, stop=ch == 1)
            ins.then_inc(s["bp_mm"], 1)

            def tiny(after_, value, rhs, col, done):
                pe.wait_ge(s[after_], value)
                nc.tensor.matmul(small[:, col:col + 2], group[:, :], rhs, start=True, stop=True).then_inc(s[done], 1)

            def embed_sub(b, e):
                k, qp = divmod(e, 2)
                i, nh = divmod(k, 2)
                w = 2 * i + qp
                pe.wait_ge(s["split_done"], 32 * b + e + 1)
                pe.wait_ge(s["we_done"], 16 * b + w + 1)
                if e == 0 and not first(b):
                    pe.wait_ge(s["x1_done"], 32 * b)
                if e == 0 and first(b):
                    pe.wait_ge(s["tab_done"], 8)
                wr = w_ring[:, w % 4, :].rearrange("c (t q o) -> c t q o", t=2, o=C)
                for q in range(2):
                    for oh in range(2):
                        for t, (wt, xt) in enumerate(((0, 0), (0, 1), (1, 0))):
                            ins = nc.tensor.matmul(PS[oh][:, 512 * nh:512 * nh + 512], wr[:, wt, q, 128 * oh:128 * oh + 128],
                                                   x_split[:, e % 2, xt, q, :],
                                                   start=(i == 0 and qp == 0 and q == 0 and t == 0),
                                                   stop=(i == 7 and qp == 1 and q == 1 and t == 2))
                ins.then_inc(s["split_used"], 1)

            def attention(b, nxt):
                pe.wait_ge(s["z_done"], 2 * b + 2)
                pe.wait_ge(s["wqkv_in"], 16 * b + 16)
                for n in range(4):
                    if n >= 2:
                        pe.wait_ge(s["qk_done"], 4 * b + n - 1)
                    i, col = n, 128 * HALF[n]
                    for nh in range(2):
                        for ch in range(2):
                            ins = nc.tensor.matmul(PS[i % 2][:, 512 * nh:512 * nh + 512], w_qkv[:, ch, col:col + 128],
                                                   z[:, ch, 512 * nh:512 * nh + 512], start=ch == 0, stop=ch == 1)
                    ins.then_inc(s["qk_mm"], 1)
                for i in range(2):
                    pe.wait_ge(s["qk_done"], 4 * b + 3 + i)
                    for t in range(4):
                        mt = 4 * i + t
                        for ch in range(2):
                            ins = nc.tensor.matmul(PS[i][:, 256 * t:256 * t + 256], z[:, ch, 128 * mt:128 * mt + 128],
                                                   w_qkv[:, ch, 512:768], start=ch == 0 , stop=ch == 1)
                    ins.then_inc(s["v_mm"], 1)

                def score_max(j, t):
                    hd, nt = divmod(t, 8)
                    h = 2 * j + hd
                    if j > 0:
                        pe.wait_ge(s["max_done"], 64 * b + 16 * j + t)
                    elif t >= 3:
                        pe.wait_ge(s["max_done"], 64 * b + t - 2)
                    elif t >= 1:
                        pe.wait_ge(s["v_done"], 2 * b + 3 - t)
                    elif positive(b):
                        pe.wait_ge(s["spec_done"], 2 * b)
                    for mh in range(2):
                        ins = nc.tensor.matmul(max_bank(j, t)[:, 512 * mh:512 * mh + 512], q_stack[0:96, h, 128 * nt:128 * nt + 128],
                                               k_stack[0:96, h, 512 * mh:512 * mh + 512], start=True, stop=True)
                    ins.then_inc(s["smax_mm"], 1)

                def transpose_max(j):
                    pe.wait_ge(s["max_done"], 64 * b + 16 * j + 16)
                    nc.tensor.transpose(PS[2][0:16, 0:128], mx[:, j % 2, :], ident[:, :].bitcast(f32)).then_inc(s["tr_mm"], 1)

                def scores(j, step):
                    nh, mt = divmod(step, 8)
                    n = 16 * j + step
                    if n >= 2:
                        pe.wait_ge(s["exp_done"], 64 * b + n - 1)
                    else:
                        pe.wait_ge(s["v_done"], 2 * b + 2)
                    off = (HP - 4 - 4 * mt) * WP_ + 512 * nh
                    for hd in range(2):
                        h = 2 * j + hd
                        at = PS[n % 2][:, 512 * hd:512 * hd + 512]
                        nc.tensor.matmul(at, k_stack[0:97, h, 128 * mt:128 * mt + 128],
                                         q_stack[0:97, h, 512 * nh:512 * nh + 512], start=True, stop=False)
                        for t in range(2):
                            ins = nc.tensor.matmul(at, ident[:, :], bias_t[:, j % 2, hd, t, off:off + 512],
                                                   start=False, stop=t == 1)
                    ins.then_inc(s["score_mm"], 1)

                def values(j, step):
                    nh, mt = divmod(step, 8)
                    n = 16 * j + step
                    pe.wait_ge(s["exp_done"], 64 * b + n + 1)
                    if mt == 0 and n >= 16:
                        pe.wait_ge(s["o_done"], 8 * b + 2 * (j - 1) + nh + 1)
                    if mt == 0 and (nh or j):
                        pe.wait_ge(s["rows_done"], 16 * b + 4 * j + 2 * nh)
                    for hd in range(2):
                        ins = nc.tensor.matmul(PB[nh][64 * hd:64 * hd + 64, :], v[:, mt, 2 * j + hd, :],
                                               prob[:, n % 2, 512 * hd:512 * hd + 512], start=mt == 0, stop=mt == 7)
                    ins.then_inc(s["prob_used"], 1)

                pe.wait_ge(s["stack_in0"], 32 * b + 32)
                pe.wait_ge(s["low_done"], 16 * b + 8)
                for t in range(16):
                    score_max(0, t)
                transpose_max(0)
                pe.wait_ge(s["kone_done"], b + 1)
                pe.wait_ge(s["ones_done"], b + 1)
                for j in range(4):
                    pe.wait_ge(s[f"bias_in{j % 2}"], 32 * (2 * b + j // 2 + 1))
                    pe.wait_ge(s["nmax_in"], 16 * (4 * b + j + 1))
                    done = 0
                    for step in range(16):
                        scores(j, step)
                        if j < 3:
                            want = max_tiles(step)
                            if done == 0:
                                pe.wait_ge(s["nmax_done"], 4 * b + j + 1)
                            if done == 0 and j == 1:
                                pe.wait_ge(s["stack_in1"], 32 * b + 32)
                                pe.wait_ge(s["low_done"], 16 * b + 16)
                            if done < want:
                                score_max(j + 1, done)
                                done += 1
                        if step or j:
                            values(*divmod(16 * j + step - 1, 16))
                        if j < 3 and done < want:
                            score_max(j + 1, done)
                            done += 1
                        if j < 3 and step == 14:
                            transpose_max(j + 1)
                        if step in UNIT_STEPS:
                            unit(b, 4 * j + UNIT_STEPS.index(step))
                values(3, 15)
                if nxt:
                    pe.wait_ge(s["nmax_done"], 4 * b + 4)
                    tiny("stat_done", 2 * b + 4, mv[:, :, 0], 0, "gm_mm")
                pe.wait_ge(s["proj_in"], 16 * b + 32)
                pe.wait_ge(s["o_done"], 8 * b + 7)
                pe.wait_ge(s["exp_done"], 64 * b + 64)
                for nh in range(2):
                    if nh == 1:
                        if nxt:
                            tiny("dev_done", 4 * b + 8, var, 2, "gv_mm")
                        pe.wait_ge(s["o_done"], 8 * b + 8)
                    for oh in range(2):
                        for ch in range(2):
                            ins = nc.tensor.matmul(PS[oh][:, 512 * nh:512 * nh + 512], w_proj[:, ch, 128 * oh:128 * oh + 128],
                                                   z[:, ch, 512 * nh:512 * nh + 512], start=ch == 0, stop=ch == 1)
                        if nh == 1:
                            ins.then_inc(s["proj_mm"], 1)

            def un_group(b, g):
                oh, p, q = g // 16, g // 4 % 4, g % 4
                w = 2 * (g // 4) + q // 2
                sl = w % 4
                if g < 2:
                    pe.wait_ge(s["z2_done"], 2 * b + 2)
                else:
                    pe.wait_ge(s["x1_done"], 32 * b + g - 1)
                pe.wait_ge(s["wu_done"], 16 * b + w + 1)
                wr = w_ring[:, sl, :].rearrange("c (t k q o) -> c t k q o", t=2, k=2, q=2)
                for nh in range(2):
                    for ch in range(2):
                        for t, (wt, zt) in enumerate(((0, 0), (0, 1), (1, 0))):
                            ins = nc.tensor.matmul(PS[g % 2][:, 512 * nh:512 * nh + 512], wr[:, wt, ch, q % 2, :],
                                                   z2[:, zt, ch, 512 * nh:512 * nh + 512],
                                                   start=ch == 0 and t == 0, stop=ch == 1 and t == 2)
                ins.then_inc(s["un_mm"], 1)

            def unit(b, n):
                if n % 2:
                    pe.wait_ge(s["rows_done"], 16 * b + n)
                elif n > 0:
                    pe.wait_ge(s["o_done"], 8 * b + n // 2)
                for j in range(2):
                    pe.wait_ge(s[f"rows_in{j}"], 16 * (16 * b + n + 1))
                    for i in range(2):
                        t = 2 * j + i
                        ins = nc.tensor.matmul(unit_bank(n)[32 * t:32 * t + 32, :], cos_h[:, :],
                                               x_rows[:, j, 4 * i:4 * i + 4, :].rearrange("h c w -> h (c w)"),
                                               start=True, stop=True)
                    ins.then_inc(s["rows_mm"], 1)

            def turn_z2(b):
                pe.wait_ge(s["z2_done"], 2 * b + 2)
                pe.wait_ge(s["rows_done"], 16 * b + 16)
                for t in range(8):
                    at = PS[2][:, C * t:C * t + C] if t < 4 else PB[(t - 4) // 2][:, C * (t % 2):C * (t % 2) + C]
                    for ch in range(2):
                        for hl in range(2):
                            ins = nc.tensor.matmul(at[:, 128 * ch:128 * ch + 128], z2[:, hl, ch, 128 * t:128 * t + 128],
                                                   ident[:, :], start=hl == 0, stop=hl == 1)
                    if t in (3, 5, 7):
                        ins.then_inc(s["z2t_mm"], 1)

            def z2_sums(b):
                pe.wait_ge(s["z2t_done"], 3 * b + 3)
                pe.wait_ge(s["gate_in"], 48 * b + 48)
                for ch in range(2):
                    for t in range(8):
                        ins = nc.tensor.matmul(PB[1][:, 64 * ch:64 * ch + 64], z2t[:, t, 128 * ch:128 * ch + 128],
                                               basis[:, t, :], start=t == 0, stop=t == 7)
                ins.then_inc(s["zf_mm"], 1)

            def y_sums(b, g):
                oh, p, q = g // 16, g // 4 % 4, g % 4
                sl = g // 2 % 4
                if g == 0:
                    pe.wait_ge(s["zf_done"], b + 1)
                wr = w_ring[:, sl, :].rearrange("c (t k q o) -> c t k q o", t=2, k=2, q=2)
                for ch in range(2):
                    for wt in (0, 1) if ch == 0 else (1, 0):
                        zs = zf[:, ch, g % 16, 0:2 - wt, :].rearrange("p t f -> p (t f)")
                        ins = nc.tensor.matmul(PB[0][:, 8 * oh:8 * oh + 8 - 4 * wt], wr[:, wt, ch, q % 2, :], zs,
                                               start=g % 16 == 0 and ch == 0 and wt == 0,
                                               stop=g % 16 == 15 and ch == 1 and wt == 0)
                ins.then_inc(s["wu_used"], 1)

            def gate_mm(b, step):
                if step == 0:
                    tiny("mv1_done", 2 * b + 2, mv[:, :, 0], 4, "gm1_mm")
                elif step == 1:
                    tiny("dev1_done", 4 * b + 4, var, 6, "gv1_mm")
                elif step == 2:
                    pe.wait_ge(s["spec_done"], 2 * b + 1)
                    for ch in range(2):
                        ins = nc.tensor.matmul(small[0:HID, 16:20], mlp1[:, ch, :], spec[:, ch, :], start=ch == 0, stop=ch == 1)
                    ins.then_inc(s["y1_mm"], 1)
                else:
                    pe.wait_ge(s["hid1_done"], b + 1)
                    for oh in range(2):
                        ins = nc.tensor.matmul(small[:, 24 + 4 * oh:28 + 4 * oh], mlp2[:, 128 * oh:128 * oh + 128], hidden,
                                               start=True, stop=True)
                    ins.then_inc(s["y2_mm"], 1)

            def after(b, nxt):
                turn_z2(b)
                for g in range(32):
                    un_group(b, g)
                    if g == 1:
                        z2_sums(b)
                    if g >= 4:
                        y_sums(b, g - 4)
                for g in range(28, 32):
                    y_sums(b, g)
                for k in range(32):
                    if nxt:
                        embed_sub(b + 1, k)
                    if k in (0, 1, 4, 6):
                        gate_mm(b, (0, 1, 4, 6).index(k))

            pe.wait_ge(s["prep"], 1)
            tiny("stat_done", 2, mv[:, :, 0], 0, "gm_mm")
            tiny("dev_done", 4, var, 2, "gv_mm")
            for e in range(32):
                embed_sub(0, e)

            def batch(b, nxt):
                attention(b, nxt)
                after(b, nxt)

            batches(pe, batch)


def kernel(**inputs):
    import math
    import numpy as np
    import concourse.bacc as bacc
    from concourse.bass_utils import run_bass_kernel_spmd

    def dct_rows(n):
        i = np.arange(n, dtype=np.float32)[:, None]
        j = np.arange(n, dtype=np.float32)[None, :]
        m = np.cos(math.pi * j * (2.0 * i + 1.0) / (2.0 * n)) * math.sqrt(2.0 / n)
        m[0] *= math.sqrt(0.5)
        return m[0:2].astype(np.float32)

    g = {k: np.asarray(v) for k, v in inputs.items()}
    c = np.ascontiguousarray

    def columns(vec):
        return c(vec.reshape(-1, 128).T)

    ah, aw = dct_rows(H), dct_rows(W)
    cos_h = np.zeros((H, 32), np.float32)
    cos_h[:, 0:2] = ah.T
    r = (np.arange(REL, dtype=np.float32) - np.float32(HP - 1)) / np.float32(HP - 1)
    grid = np.einsum("uhp,vwq->hwpquv", ah.reshape(2, HP, PT), aw.reshape(2, WP_, PT)).reshape(8, 128, 4 * PT * PT)
    rel = np.stack([np.repeat(r, REL), np.tile(r, REL), np.ones(REL * REL, np.float32)])
    arrays = {
        "x": g["x"],
        "w_embed": c(g["L0_conv_w_embed"].reshape(C, 2, 128, PT, 2, 2).transpose(1, 3, 4, 2, 5, 0)).reshape(16, 128, 512),
        "w_unembed": c(g["L0_conv_w_unembed"].reshape(2, 128, 2, 128, PT, 2, 2).transpose(2, 4, 5, 1, 0, 6, 3)
                       ).reshape(16, 128, 512),
        "w_qkvt": c(g["L0_conv_w_qkv"].T), "w_projt": c(g["L0_conv_w_proj"].T),
        "b_embed": columns(g["L0_conv_b_embed"]), "b_unembed": columns(g["L0_conv_b_unembed"]),
        "b_proj": columns(g["L0_conv_b_proj"]), "b_v": columns(g["L0_conv_b_qkv"][2 * C:]),
        "b_qk": columns(g["L0_conv_b_qkv"][:2 * C]),
        "cpb_w1t": c(g["L0_conv_cpb_w1"].T), "cpb_b1": g["L0_conv_cpb_b1"].reshape(1, CPB),
        "cpb_w2t": c(g["L0_conv_cpb_w2"].T),
        "w1t": c(g["L1_conv_w1"].T), "w2t": c(g["L1_conv_w2"].T),
        "identity": np.eye(128, dtype=np.float32),
        "group_mean": np.kron(np.eye(16, dtype=np.float32), np.full((8, 8), 0.125, np.float32)),
        "basis": c(grid.transpose(1, 0, 2)), "cos_h": cos_h, "cos_w": c(np.broadcast_to(aw[None], (128, 2, W))), "rel": rel,
    }
    sums = [float(ah[u].astype(np.float64).sum() * aw[w].astype(np.float64).sum()) for u in range(2) for w in range(2)]
    nc = bacc.Bacc("TRN2", target_bir_lowering=False, num_devices=1)
    aps = {k: nc.dram_tensor("in_" + k, v.shape, mybir.dt.from_np(v.dtype), kind="ExternalInput").ap()
           for k, v in arrays.items()}
    aps["out"] = nc.dram_tensor("x_out", (B, C, H, W), mybir.dt.float32, kind="ExternalOutput").ap()
    build(nc, aps, sums)
    res = run_bass_kernel_spmd(nc, [{"in_" + k: v for k, v in arrays.items()}], core_ids=[0])
    return res.results[0]["x_out"]
```
